# Optimizing a Trainium2 kernel written in Bass

```python
import numpy as np
import jax
import jax.numpy as jnp

def _softmax(x, axis=-1):
    return jax.nn.softmax(x, axis=axis)

def _gelu(x):
    return jax.nn.gelu(x, approximate=True)

def _silu(x):
    return jax.nn.silu(x)

def _sigmoid(x):
    return jax.nn.sigmoid(x)

def _layernorm(x, axis=-1, eps=1e-05):
    m = jnp.mean(x, axis=axis, keepdims=True)
    v = jnp.var(x, axis=axis, keepdims=True)
    return (x - m) / jnp.sqrt(v + eps)

def _scatter_add(tgt, idx, src, axis=0):
    return tgt.at[idx].add(src)

def _segment_sum(src, seg, n):
    return jax.ops.segment_sum(src, seg, n)
kernel_name = 'mk_decoder_preln_d1_seqx_r2_166523'

def setup_inputs(seed: int=0):
    np.random.seed(seed)
    _w = jnp.asarray

    def _rec_inputs():
        import jax
        import jax.numpy as jnp
        _rk = jax.random.key(seed)
        x = 7.22e-05 + 1 * jax.random.normal(jax.random.fold_in(_rk, 1), (16, 256, 1024), jnp.float32)
        _lenS = 256 - jax.random.randint(jax.random.fold_in(_rk, 7), (16,), 0, max(1, 256 // 4) + 1, jnp.int32)
        _lenS2 = 256 - jax.random.randint(jax.random.fold_in(_rk, 8), (16,), 0, max(1, 256 // 4) + 1, jnp.int32)
        _ctx_2048P = jax.random.normal(jax.random.fold_in(_rk, 11), (16, 16, 1024), jnp.float32)
        _ctx_2048c = jax.random.dirichlet(jax.random.fold_in(_rk, 511), 0.3 * jnp.ones((16,), jnp.float32), (16, 256))
        _ctx_2048t = jnp.einsum('bsk,bkd->bsd', _ctx_2048c, _ctx_2048P)
        _ctx_2048t = _ctx_2048t * jax.lax.rsqrt(jnp.mean(jnp.square(_ctx_2048t)) + 1e-12) * 0.953939
        ctx_2048 = 4.13588e-05 + 0.999923 * (_ctx_2048t + 0.3 * jax.random.normal(jax.random.fold_in(_rk, 611), (16, 256, 1024), jnp.float32))
        return (x, ctx_2048)
    x, ctx_2048 = _rec_inputs()

    def _L0_attn_setup():
        import jax, jax.numpy as jnp
        import numpy as np
        DIM = 1024
        N_HEADS = 16
        HEAD_DIM = DIM // N_HEADS
        GROUP_SIZE = 128
        THRESHOLD = 0.5
        EPS = 1e-08
        B, T = (2, 1024)

        def _ternary_dequant(w):
            O, I = w.shape
            g = I // GROUP_SIZE
            wg = w.reshape(O, g, GROUP_SIZE)
            scale = jnp.clip(jnp.mean(jnp.abs(wg), axis=-1, keepdims=True), EPS)
            wn = wg / scale
            q = jnp.where(wn > THRESHOLD, 1.0, jnp.where(wn < -THRESHOLD, -1.0, 0.0))
            return (q * scale).reshape(O, I)

        def _bitlinear(x, w):
            w_ste = w + jax.lax.stop_gradient(_ternary_dequant(w) - w)
            return x @ w_ste.T

        def _rope_tables(t, head_dim, base=10000.0):
            half = head_dim // 2
            inv_freq = 1.0 / base ** (jnp.arange(half, dtype=jnp.float32) / half)
            freqs = jnp.outer(jnp.arange(t, dtype=jnp.float32), inv_freq)
            return (jnp.cos(freqs), jnp.sin(freqs))

        def _apply_rope(x, cos, sin):
            d = x.shape[-1]
            x1, x2 = (x[..., :d // 2], x[..., d // 2:])
            cos = cos[None, None, :, :]
            sin = sin[None, None, :, :]
            return jnp.concatenate([x1 * cos - x2 * sin, x1 * sin + x2 * cos], axis=-1)
        key = jax.random.key(seed)
        ks = jax.random.split(key, 5)
        std = 1.0 / np.sqrt(DIM)
        return {'x': jax.random.normal(ks[0], (B, T, DIM), dtype=jnp.float32), 'w_q': jax.random.normal(ks[1], (DIM, DIM), dtype=jnp.float32) * std, 'w_k': jax.random.normal(ks[2], (DIM, DIM), dtype=jnp.float32) * std, 'w_v': jax.random.normal(ks[3], (DIM, DIM), dtype=jnp.float32) * std, 'w_o': jax.random.normal(ks[4], (DIM, DIM), dtype=jnp.float32) * std}
    _L0_attn_all = _L0_attn_setup()
    _L0_attn_in = {k: v for k, v in _L0_attn_all.items() if k in ('w_q', 'w_k', 'w_v', 'w_o')}
    del _L0_attn_all

    def _L0_xattn_setup():
        import math
        import jax, jax.numpy as jnp
        import numpy as np
        HEADS = 16
        MASKED_BIAS = -10000.0

        def _mha(q, k, v):
            B, Sq, D = q.shape
            Sk = k.shape[-2]
            hd = D // HEADS
            qh = q.reshape(B, Sq, HEADS, hd).transpose(0, 2, 1, 3)
            kh = k.reshape(B, Sk, HEADS, hd).transpose(0, 2, 1, 3)
            vh = v.reshape(B, Sk, HEADS, hd).transpose(0, 2, 1, 3)
            scores = jnp.einsum('bhqd,bhkd->bhqk', qh, kh) / math.sqrt(hd)
            qi = jnp.arange(Sq)[:, None] + (Sk - Sq)
            ki = jnp.arange(Sk)[None, :]
            causal = ki <= qi
            scores = jnp.where(causal[None, None], scores, jnp.asarray(MASKED_BIAS, scores.dtype))
            attn = jax.nn.softmax(scores, axis=-1)
            out = jnp.einsum('bhqk,bhkd->bhqd', attn, vh)
            return out.transpose(0, 2, 1, 3).reshape(B, Sq, D)
        key = jax.random.key(seed)
        kq, kk, kv = jax.random.split(key, 3)
        B, S, D = (4, 512, 1024)
        q = jax.random.normal(kq, (B, S, D), dtype=jnp.float32)
        k = jax.random.normal(kk, (B, S, D), dtype=jnp.float32)
        v = jax.random.normal(kv, (B, S, D), dtype=jnp.float32)
        return {'q': q, 'k': k, 'v': v}
    _L0_xattn_all = _L0_xattn_setup()
    _L0_xattn_in = {k: v for k, v in _L0_xattn_all.items() if k in ()}
    del _L0_xattn_all

    def _L0_ffn_setup():
        import jax, jax.numpy as jnp
        import numpy as np
        RANK = 64
        SCALING = 1.0 / RANK
        TEMPERATURE = 1.0
        key = jax.random.key(seed)
        k_x, k_a, k_b, k_w = jax.random.split(key, 4)
        B_, S, D = (4, 1024, 1024)
        E, R, O = (8, RANK, 1024)
        x = jax.random.normal(k_x, (B_, S, D), dtype=jnp.float32)
        A = jax.random.normal(k_a, (E, R, D), dtype=jnp.float32) * (1.0 / np.sqrt(D))
        Bw = jax.random.normal(k_b, (E, O, R), dtype=jnp.float32) * 0.02
        Wr = jax.random.normal(k_w, (E, D), dtype=jnp.float32) * (1.0 / np.sqrt(D))
        br = jnp.zeros((E,), dtype=jnp.float32)
        return {'x': x, 'A': A, 'B': Bw, 'Wr': Wr, 'br': br}
    _L0_ffn_all = _L0_ffn_setup()
    _L0_ffn_in = {k: v for k, v in _L0_ffn_all.items() if k in ('A', 'B', 'Wr', 'br')}
    del _L0_ffn_all
    return {'x': x, 'ctx_2048': ctx_2048, 'L0_attn_w_q': _L0_attn_in['w_q'], 'L0_attn_w_k': _L0_attn_in['w_k'], 'L0_attn_w_v': _L0_attn_in['w_v'], 'L0_attn_w_o': _L0_attn_in['w_o'], 'L0_ffn_A': _L0_ffn_in['A'], 'L0_ffn_B': _L0_ffn_in['B'], 'L0_ffn_Wr': _L0_ffn_in['Wr'], 'L0_ffn_br': _L0_ffn_in['br']}

def reference(x, ctx_2048, L0_attn_w_q, L0_attn_w_k, L0_attn_w_v, L0_attn_w_o, L0_ffn_A, L0_ffn_B, L0_ffn_Wr, L0_ffn_br):
    import jax
    import jax.numpy as jnp

    def _L0_attn_ref(x, w_q, w_k, w_v, w_o):
        import jax, jax.numpy as jnp
        import numpy as np
        DIM = 1024
        N_HEADS = 16
        HEAD_DIM = DIM // N_HEADS
        GROUP_SIZE = 128
        THRESHOLD = 0.5
        EPS = 1e-08
        B, T = (2, 1024)

        def _ternary_dequant(w):
            O, I = w.shape
            g = I // GROUP_SIZE
            wg = w.reshape(O, g, GROUP_SIZE)
            scale = jnp.clip(jnp.mean(jnp.abs(wg), axis=-1, keepdims=True), EPS)
            wn = wg / scale
            q = jnp.where(wn > THRESHOLD, 1.0, jnp.where(wn < -THRESHOLD, -1.0, 0.0))
            return (q * scale).reshape(O, I)

        def _bitlinear(x, w):
            w_ste = w + jax.lax.stop_gradient(_ternary_dequant(w) - w)
            return x @ w_ste.T

        def _rope_tables(t, head_dim, base=10000.0):
            half = head_dim // 2
            inv_freq = 1.0 / base ** (jnp.arange(half, dtype=jnp.float32) / half)
            freqs = jnp.outer(jnp.arange(t, dtype=jnp.float32), inv_freq)
            return (jnp.cos(freqs), jnp.sin(freqs))

        def _apply_rope(x, cos, sin):
            d = x.shape[-1]
            x1, x2 = (x[..., :d // 2], x[..., d // 2:])
            cos = cos[None, None, :, :]
            sin = sin[None, None, :, :]
            return jnp.concatenate([x1 * cos - x2 * sin, x1 * sin + x2 * cos], axis=-1)
        b, t, c = x.shape
        scale = HEAD_DIM ** (-0.5)

        def split_heads(y):
            return y.reshape(b, t, N_HEADS, HEAD_DIM).transpose(0, 2, 1, 3)
        q = split_heads(_bitlinear(x, w_q))
        k = split_heads(_bitlinear(x, w_k))
        v = split_heads(_bitlinear(x, w_v))
        cos, sin = _rope_tables(t, HEAD_DIM)
        q = _apply_rope(q, cos, sin)
        k = _apply_rope(k, cos, sin)
        scores = jnp.einsum('bhqd,bhkd->bhqk', q, k) * scale
        causal = jnp.triu(jnp.ones((t, t), dtype=bool), k=1)
        scores = jnp.where(causal[None, None], -jnp.inf, scores)
        probs = jax.nn.softmax(scores, axis=-1)
        y = jnp.einsum('bhqk,bhkd->bhqd', probs, v)
        y = y.transpose(0, 2, 1, 3).reshape(b, t, c)
        return _bitlinear(y, w_o)

    def _L0_xattn_ref(q, k, v):
        import math
        import jax, jax.numpy as jnp
        import numpy as np
        HEADS = 16
        MASKED_BIAS = -10000.0

        def _mha(q, k, v):
            B, Sq, D = q.shape
            Sk = k.shape[-2]
            hd = D // HEADS
            qh = q.reshape(B, Sq, HEADS, hd).transpose(0, 2, 1, 3)
            kh = k.reshape(B, Sk, HEADS, hd).transpose(0, 2, 1, 3)
            vh = v.reshape(B, Sk, HEADS, hd).transpose(0, 2, 1, 3)
            scores = jnp.einsum('bhqd,bhkd->bhqk', qh, kh) / math.sqrt(hd)
            qi = jnp.arange(Sq)[:, None] + (Sk - Sq)
            ki = jnp.arange(Sk)[None, :]
            causal = ki <= qi
            scores = jnp.where(causal[None, None], scores, jnp.asarray(MASKED_BIAS, scores.dtype))
            attn = jax.nn.softmax(scores, axis=-1)
            out = jnp.einsum('bhqk,bhkd->bhqd', attn, vh)
            return out.transpose(0, 2, 1, 3).reshape(B, Sq, D)
        return _mha(q, k, v)

    def _L0_ffn_ref(x, A, B, Wr, br):
        import jax, jax.numpy as jnp
        import numpy as np
        RANK = 64
        SCALING = 1.0 / RANK
        TEMPERATURE = 1.0
        batch, seq, d = x.shape
        E, out_dim = (B.shape[0], B.shape[1])
        x_flat = x.reshape(-1, d)
        logits = (x_flat @ Wr.T + br) / TEMPERATURE
        probs = jax.nn.softmax(logits, axis=-1)
        expert_idx = jnp.argmax(probs, axis=-1)
        expert_weight = jnp.max(probs, axis=-1)
        h = jnp.einsum('nd,erd->ner', x_flat, A)
        y = jnp.einsum('ner,eor->neo', h, B) * SCALING
        sel = jnp.take_along_axis(y, expert_idx[:, None, None], axis=1)[:, 0, :]
        out_flat = sel * expert_weight[:, None]
        return out_flat.reshape(batch, seq, out_dim)
    x = x + _L0_attn_ref(_layernorm(x, axis=-1), L0_attn_w_q, L0_attn_w_k, L0_attn_w_v, L0_attn_w_o)
    x = x + _L0_xattn_ref(_layernorm(x, axis=-1), ctx_2048, ctx_2048)
    x = x + _L0_ffn_ref(_layernorm(x, axis=-1), L0_ffn_A, L0_ffn_B, L0_ffn_Wr, L0_ffn_br)
    return x

_drawn_inputs = setup_inputs


def setup_inputs(seed=0):
    import zlib

    import numpy as np

    out = dict(_drawn_inputs(seed))
    spreads = {'L0_ffn_br': (0.0, 0.8)}
    factors = {'L0_ffn_A': 8.0, 'L0_ffn_B': 8.0, 'L0_ffn_Wr': 8.0}
    for name, (base, spread) in spreads.items():
        noise = np.random.default_rng([zlib.crc32(name.encode()), seed]).standard_normal(out[name].shape)
        drawn = base * np.exp(spread * noise) if base else spread * noise
        out[name] = jnp.asarray(drawn.astype(out[name].dtype))
    for name, factor in factors.items():
        out[name] = (out[name] * factor).astype(out[name].dtype)
    return out
```

```python
from contextlib import ExitStack

import numpy as np

import concourse.bass as bass
from concourse import mybir

F32 = mybir.dt.float32
F16 = mybir.dt.float16
BF16 = mybir.dt.bfloat16
ALU = mybir.AluOpType
ACT = mybir.ActivationFunctionType
AX = mybir.AxisListType

P = 128
NB = 16
T = 256
NT = T // P
D = 1024
DT = D // P
H = 16
HD = D // H
NPAIR = H // 2
GROUP = 128
NG = D // GROUP
BANK = 512
NJ = 3
PVW = HD + 2
E = 8
R = 64
ER = E * R
ERT = ER // P
MASK = -1e30
W_SCALE = 256.0
E_SCALE = 64.0
LN_EPS = 1e-5
SCALE_EPS = 1e-8


def make_identity(pool, ident, ident_h, mask, done):
    pool.memset(ident[:], 0.0).then_inc(done, 1)
    pool.memset(mask[:], 0.0).then_inc(done, 1)
    pool.wait_ge(done, 2)
    pool.affine_select(out=ident[:], in_=ident[:], compare_op=ALU.not_equal, fill=1.0, base=0,
                       pattern=[[-1, P]], channel_multiplier=1).then_inc(done, 1)
    pool.affine_select(out=mask[:], in_=mask[:], compare_op=ALU.is_ge, fill=MASK, base=0,
                       pattern=[[-1, P]], channel_multiplier=1).then_inc(done, 1)
    pool.wait_ge(done, 3)
    pool.tensor_copy(ident_h[:], ident[:]).then_inc(done, 1)


IDENT_DONE = 5


def split_product(pe, out, lhs, rhs, n_tiles):
    for a in range(n_tiles):
        for k, (i, j) in enumerate(((0, 1), (1, 0), (0, 0))):
            last = pe.matmul(out, lhs(i, a), rhs(j, a), start=a == 0 and k == 0,
                             stop=a == n_tiles - 1 and k == 2)
    return last


def causal_scores(pe, banks, q, k, ident_h, mask, done):
    rows = [slice(HD * e, HD * e + HD) for e in range(2)]
    for i, j in ((0, 1), (1, 0), (0, 0)):
        for e in range(2):
            pe.matmul(banks[e][:, 0:P], q(i, rows[e])[:, 0:P], k(j, rows[e])[:, 0:P],
                      start=(i, j) == (0, 1), stop=False)
    for e in range(2):
        pe.matmul(banks[e][:, 0:P], ident_h[:], mask[:], start=False, stop=True)
    for i, j in ((0, 1), (1, 0), (0, 0)):
        for e in range(2):
            pe.matmul(banks[e][:, P:3 * P], q(i, rows[e])[:, P:T], k(j, rows[e]),
                      start=(i, j) == (0, 1), stop=False)
    for e in range(2):
        pe.matmul(banks[e][:, 2 * P:3 * P], ident_h[:], mask[:], start=False, stop=True) \
            .then_inc(done, 1)


def weights_times_values(pe, out, pT, v, h):
    for q, blocks in ((0, ((0, 0),)), (1, ((1, 0), (2, 1)))):
        for b, kt in blocks:
            for i, j in ((1, 0), (0, 1), (0, 0)):
                last = pe.matmul(out[:, q, 0:HD + 1], pT(i, b), v[:, j, kt, h, :],
                                 start=(i, j) == (1, 0) and kt == 0,
                                 stop=(i, j) == (0, 0) and b == blocks[-1][0])
    return last


def program(nc, x, ctx, w_q, w_k, w_v, w_o, A, B, Wr, br, rope_cos, rope_sin, out):
    scratch = nc.dram_tensor("after_self_attention", (NB + 1, T, D), F32, kind="Internal").ap()

    with ExitStack() as st:
        def sb(name, shape, dt=F32):
            return st.enter_context(nc.sbuf_tensor(name, shape, dt))

        ident = sb("ident", [P, P])
        ident_h = sb("ident_h", [P, P], BF16)
        mask = sb("mask", [P, P], BF16)
        ps_j = [st.enter_context(nc.psum_tensor(f"ps_j{k}", [P, BANK], F32)) for k in range(NJ)]
        ps_s = [st.enter_context(nc.psum_tensor(f"ps_s{k}", [P, BANK], F32)) for k in range(2)]
        ps_t = [st.enter_context(nc.psum_tensor(f"ps_t{k}", [P, BANK], F32)) for k in range(2)]
        ps_o = st.enter_context(nc.psum_tensor("ps_o", [P, BANK], F32))
        banks = (ps_j, ps_s, ps_t, ps_o)
        consts = (ident, ident_h, mask)
        with ExitStack() as st1:
            wT = [st1.enter_context(nc.sbuf_tensor(f"wT{m}", [P, 2, DT, D], F16))
                  for m in range(4)]
            weights(nc, consts, banks, wT, (w_q, w_k, w_v, w_o))
            self_attention(nc, consts, banks, wT, x, rope_cos, rope_sin, scratch)
        second_half(nc, consts, banks, A, B, Wr, br, scratch, ctx, out)


def weights(nc, consts, banks, wT, mats):
    ident, ident_h, mask = consts
    ps_j, ps_s, ps_t, ps_o = banks
    sets = [[ps_j[0], ps_j[1], ps_j[2], ps_s[0]], [ps_s[1], ps_t[0], ps_t[1], ps_o]]
    NS = 4

    with ExitStack() as st:
        def sb(name, shape, dt=F32):
            return st.enter_context(nc.sbuf_tensor(name, shape, dt))

        def sem(name):
            return st.enter_context(nc.semaphore(name))
        stage = sb("stage", [P, NS, D])
        above = sb("above", [P, 2, D], F16)
        below = sb("below", [P, 2, D], F16)
        diag = sb("diag", [P, 2, 2, NG, P], F16)
        ident_16 = sb("ident_16", [P, P], F16)
        asum = sb("asum", [P, 2, NG])
        scale = sb("scale", [P, 2, NG])
        scaleW = sb("scaleW", [P, 2, NG])
        high = sb("high", [P, 2, NG], F16)
        low = sb("low", [P, 2, NG], F16)
        thr = sb("thr", [P, 2, 2, NG])
        consts_done = sem("consts_done")
        w_in = [sem(f"w_in{p}") for p in range(NS)]
        summed = sem("summed")
        scaled = sem("scaled")
        halved = sem("halved")
        low_done = sem("low_done")
        compared = sem("compared")
        signs = sem("signs")
        diag_lo = sem("diag_lo")
        diag_hi = sem("diag_hi")
        block_done = sem("block_done")
        kept = sem("kept")
        block = st.enter_context(nc.Block())

        @block.sync
        def _(sp):
            for m in range(4):
                rows = mats[m].rearrange("(k p r) i -> k p r i", p=NS, r=P)
                with sp.Fori(0, DT // NS) as k:
                    for p in range(NS):
                        n = NS * k + (DT * m + p)
                        sp.wait_ge(compared, 2 * n + 2)
                        sp.dma_start(stage[:, p, :], rows[k, p]).then_inc(w_in[p], 16)

        @block.gpsimd
        def _(pool):
            make_identity(pool, ident, ident_h, mask, consts_done)
            pool.tensor_copy(ident_16[:], ident[:]).then_inc(consts_done, 1)
            pool.wait_ge(consts_done, IDENT_DONE + 1)
            for m in range(4):
                with pool.Fori(0, DT // NS) as k:
                    for u in range(NS):
                        n, p = NS * k + (DT * m + u), u % 2
                        pool.wait_ge(low_done, n + 1)
                        pool.tensor_tensor(
                            diag[:, p, 1], ident_16[:].unsqueeze(1).broadcast_to([P, NG, P]),
                            low[:, p, :].unsqueeze(2).broadcast_to([P, NG, P]), ALU.mult) \
                            .then_inc(diag_lo, 1)
                        pool.wait_ge(compared, 2 * n + 10)
                        pool.tensor_tensor(above[:, p, :], above[:, p, :], below[:, p, :],
                                           ALU.subtract).then_inc(signs, 1)

        @block.vector
        def _(dve):
            dve.sem_inc(compared, 2 * NS)
            for m in range(4):
                with dve.Fori(0, DT // NS) as k:
                    for u in range(NS):
                        n, p = NS * k + (DT * m + u), u % 2
                        w = stage[:, u, :].rearrange("p (g i) -> p g i", g=NG)
                        dve.wait_ge(w_in[u], 16 * k + (16 * (DT // NS) * m + 16))
                        dve.tensor_reduce(asum[:, p, :], w, AX.X, ALU.add,
                                          apply_absolute_value=True).then_inc(summed, 1)
                        dve.wait_ge(block_done, n + 1)
                        dve.wait_ge(summed, n + 1)
                        dve.tensor_scalar(scale[:, p, :], asum[:, p, :], 1.0 / GROUP, SCALE_EPS,
                                          ALU.mult, ALU.max).then_inc(scaled, 1)
                        dve.wait_ge(scaled, n + 1)
                        dve.tensor_scalar(thr[:, p, 0, :], scale[:, p, :], 0.5, None,
                                          ALU.mult).then_inc(halved, 1)
                        dve.tensor_scalar(thr[:, p, 1, :], scale[:, p, :], -0.5, None,
                                          ALU.mult).then_inc(halved, 1)
                        dve.tensor_scalar(scaleW[:, p, :], scale[:, p, :], W_SCALE, None,
                                          ALU.mult).then_inc(halved, 1)
                        dve.tensor_scalar(high[:, p, :], scale[:, p, :], W_SCALE, None,
                                          ALU.mult).then_inc(halved, 1)
                        dve.wait_ge(halved, 4 * n + 4)
                        dve.tensor_tensor(low[:, p, :], scaleW[:, p, :], high[:, p, :],
                                          ALU.subtract).then_inc(low_done, 1)
                        for j, (to, op) in enumerate(((above, ALU.is_gt), (below, ALU.is_lt))):
                            dve.tensor_tensor(
                                to[:, p, :].rearrange("p (g i) -> p g i", g=NG), w,
                                thr[:, p, j, :].unsqueeze(2).broadcast_to([P, NG, GROUP]),
                                op).then_inc(compared, 1)

        @block.scalar
        def _(act):
            act.sem_inc(kept, 8)
            act.wait_ge(consts_done, IDENT_DONE)

            for m in range(4):
                with act.Fori(0, DT // NS) as k:
                    for u in range(NS):
                        n, p = NS * k + (DT * m + u), u % 2
                        act.wait_ge(halved, 4 * n + 3)
                        for g in range(NG):
                            last = act.activation(diag[:, p, 0, g, :], ident[:], ACT.Copy,
                                                  scale=scaleW[:, p, g:g + 1])
                        last.then_inc(diag_hi, 1)
                        act.wait_ge(block_done, n + 3)
                        for half in range(2):
                            for j in range(2):
                                act.activation(
                                    wT[m][:, half, 4 * j:4 * j + 4, bass.ts(NS * k + u, P)],
                                    sets[p][2 * half + j][:].rearrange("p (g o) -> p g o", g=4),
                                    ACT.Copy).then_inc(kept, 1)

        @block.tensor
        def _(pe):
            pe.sem_inc(block_done, 2)
            for m in range(4):
                with pe.Fori(0, DT // NS) as k:
                    for u in range(NS):
                        n, p = NS * k + (DT * m + u), u % 2
                        pe.wait_ge(signs, n + 1)
                        pe.wait_ge(diag_lo, n + 1)
                        pe.wait_ge(diag_hi, n + 1)
                        pe.wait_ge(kept, 4 * n + 4)
                        for half in range(2):
                            for g in range(NG):
                                last = pe.matmul(sets[p][2 * half + g // 4][:, bass.ts(g % 4, P)],
                                                 above[:, p, bass.ts(g, P)], diag[:, p, half, g, :],
                                                 start=True, stop=True)
                        last.then_inc(block_done, 1)


def self_attention(nc, consts, banks, wT, x, rope_cos, rope_sin, scratch):
    st = ExitStack()

    def sb(name, shape, dt=F32):
        return st.enter_context(nc.sbuf_tensor(name, shape, dt))
    ident, ident_h, mask = consts
    ps_j, ps_s, ps_t, ps_ob = banks
    ps_o = ps_ob[:, 0:2 * NT * PVW].rearrange("p (e n d) -> p e n d", e=2, n=NT)
    wqT, wkT, wvT, woT = wT
    xin = sb("xin", [P, NT, D])
    xT = sb("xT", [P, 2, DT, T], F16)
    xres = sb("xres", [P, NT, D])
    y = sb("y", [P, NT, D])
    yT = sb("yT", [P, 2, DT, T], F16)
    v = sb("v", [P, 2, NT, H, HD + 1], F16)
    raw = sb("raw", [P, 2, 2, T])
    swp = sb("swp", [P, 2, 2, T])
    rot = sb("rot", [P, 2, 2, T])
    qk = sb("qk", [P, 2, 2, 2, T], F16)
    prob = sb("prob", [P, 4, 3 * P])
    probT = sb("probT", [P, 2, 2, 3 * P], F16)
    negmax = sb("negmax", [P, 4, NT])
    rinv = sb("rinv", [P, 2, NT])
    cos = sb("cos", [P, 2, T])
    sin = sb("sin", [P, 2, T])
    stats = sb("stats", [P, NT, 2, 6])
    mv = sb("mv", [P, NT, 2])
    rstd = sb("rstd", [P, NT])
    nothing = sb("nothing", [P, 1])
    minus_half = sb("minus_half", [P, NT])
    x_t = x.rearrange("b (n p) d -> b p n d", p=P)
    scr_t = scratch.rearrange("b (n p) d -> b p n d", p=P)

    V0, QK0, WO, XT0, YT0, NC = 0, 4, (12, 13, 14, 19), 15, 20, 24
    FIRST = 4

    def counted(k, upto):
        return len([c for c in range(upto) if c % NJ == k and not QK0 <= c < QK0 + NPAIR])
    each = [counted(k, NC) for k in range(NJ)]
    before = [len([c for c in range(FIRST) if c % NJ == k]) for k in range(NJ)]

    with st:
        def sem(name):
            return st.enter_context(nc.semaphore(name))
        x_in = sem("x_in")
        res_in = sem("res_in")
        x1_out = sem("x1_out")
        swapped = [sem(f"swapped{p}") for p in range(2)]
        j_ready = sem("j_ready")
        j_free = [sem(f"j_free{k}") for k in range(NJ)]
        raw_done = sem("raw_done")
        cos_done = sem("cos_done")
        sin_done = sem("sin_done")
        rot_done = sem("rot_done")
        qk_hi = sem("qk_hi")
        qk_done = sem("qk_done")
        s_ready = sem("s_ready")
        max_done = sem("max_done")
        exp_done = sem("exp_done")
        pT_ready = sem("pT_ready")
        pT_hi = sem("pT_hi")
        pT_done = sem("pT_done")
        hi_done = sem("hi_done")
        v_hi = sem("v_hi")
        o_ready = sem("o_ready")
        recip_done = sem("recip_done")
        y_done = sem("y_done")
        ln_stat = sem("ln_stat")
        ln_pow = sem("ln_pow")
        ln_done = sem("ln_done")
        y_zero = sem("y_zero")
        zeroed = sem("zeroed")
        consts_in = sem("consts_in")
        block = st.enter_context(nc.Block())

        def bank_of(c):
            return ps_j[c % NJ]

        def freed(i, c):
            if QK0 <= c < QK0 + NPAIR:
                return raw_done, NPAIR * i + (c - QK0 + 1)
            return j_free[c % NJ], each[c % NJ] * i + (before[c % NJ] + counted(c % NJ, c + 1))

        @block.sync
        def _(sp):
            sp.dma_start(xin[:], x_t[0]).then_inc(x_in, 16)
            sp.dma_start(xres[:], x_t[0]).then_inc(res_in, 16)
            sp.dma_start(cos[:], rope_cos).then_inc(consts_in, 16)
            sp.dma_start(sin[:], rope_sin).then_inc(consts_in, 16)
            with sp.Fori(0, NB) as i:
                sp.wait_ge(j_ready, NC * i + (FIRST + V0 + 1))
                sp.dma_start(xin[:], x_t[(i + 1) % NB]).then_inc(x_in, 16)
                for t in range(NPAIR):
                    p = t % 2
                    sp.wait_ge(raw_done, NPAIR * i + (t + 1))
                    sp.wait_ge(qk_done, NPAIR * i + (t + 1))
                    for a in range(4):
                        b = a ^ 1
                        sp.dma_start(swp[32 * a:32 * a + 32, p], raw[32 * b:32 * b + 32, p]) \
                            .then_inc(swapped[p], 16)
                sp.wait_ge(*freed(i, WO[3]))
                sp.dma_start(scr_t[i], xres[:]).then_inc(x1_out, 16)
                sp.wait_ge(x1_out, 16 * i + 16)
                sp.dma_start(xres[:], x_t[i]).then_inc(res_in, 16)
            sp.wait_ge(j_free[0], each[0] * NB + (before[0] + 2))
            sp.dma_start(scr_t[NB], xres[:]).then_inc(x1_out, 16)
            sp.wait_ge(x1_out, 16 * NB + 16)

        @block.tensor
        def _(pe):
            def transposes(src, c, i):
                for a in range(2):
                    for n in range(NT):
                        last = pe.transpose(bank_of(c)[:, bass.ts(a * NT + n, P)],
                                            src[:, n, bass.ts((c - i) * 2 + a, P)], ident[:])
                last.then_inc(j_ready, 1)

            def out_projection(c, j):
                n, half = j // 2, j % 2
                split_product(pe, bank_of(c)[:], lambda i, a: yT[:, i, a, bass.ts(n, P)],
                              lambda i, a: woT[:, i, a, bass.ts(half, BANK)], DT) \
                    .then_inc(j_ready, 1)

            pe.wait_ge(zeroed, 3)
            pe.wait_ge(y_zero, 1)
            pe.wait_ge(ln_done, 2)
            for c in range(FIRST):
                if c >= NJ:
                    pe.wait_ge(j_free[c % NJ], 1)
                transposes(xin, c, 0)
            with pe.Fori(0, NB) as i:
                for k in range(NJ):
                    pe.wait_ge(j_free[k], each[k] * i + before[k])
                for j in range(4):
                    c = V0 + j
                    if j >= NJ:
                        pe.wait_ge(*freed(i, c - NJ))
                    split_product(pe, bank_of(c)[:], lambda i, a: xT[:, i, a, bass.ts(j // 2, P)],
                                  lambda i, a: wvT[:, i, a, bass.ts(j % 2, BANK)], DT) \
                        .then_inc(j_ready, 1)
                for s in range(NPAIR + 2):
                    if s < NPAIR:
                        c = QK0 + s
                        pe.wait_ge(*freed(i, c - NJ))
                        for w, m in enumerate((wqT, wkT)):
                            last = split_product(pe, bank_of(c)[:, bass.ts(w, T)],
                                                 lambda i, a: m[:, i, a, bass.ts(s, P)],
                                                 lambda i, a: xT[:, i, a, :], DT)
                        last.then_inc(j_ready, 1)
                    else:
                        c = WO[s - NPAIR]
                        pe.wait_ge(*freed(i, c - NJ))
                        out_projection(c, s - NPAIR)
                    if s >= 2:
                        for e in range(2):
                            h = 2 * (s - 2) + e
                            pe.wait_ge(exp_done, H * i + (2 + h + 1))
                            for k in range(3):
                                last = pe.transpose(ps_t[e][:, bass.ts(k, P)],
                                                    prob[:, h % 4, bass.ts(k, P)], ident[:])
                            last.then_inc(pT_ready, 1)
                    if 1 <= s <= NPAIR:
                        t = s - 1
                        pe.wait_ge(qk_done, NPAIR * i + (2 + t + 1))
                        pe.wait_ge(exp_done, H * i + (2 * t + 2))
                        causal_scores(pe, ps_s, lambda i, r: qk[r, t % 2, i, 0],
                                      lambda i, r: qk[r, t % 2, i, 1], ident_h, mask, s_ready)
                    if s >= 2:
                        t = s - 2
                        pe.wait_ge(y_done, NPAIR * i + (t + 1))
                        for e in range(2):
                            pe.wait_ge(pT_done, H * i + (2 * t + e + 1))
                            last = weights_times_values(
                                pe, ps_o[:, e], lambda i, b: probT[:, e, i, bass.ts(b, P)],
                                v, 2 * t + e)
                        last.then_inc(o_ready, 1)
                pe.wait_ge(*freed(i, WO[2] - NJ))
                out_projection(WO[2], 2)
                pe.wait_ge(ln_done, 2 * i + 4)
                for c in range(XT0, XT0 + 4):
                    pe.wait_ge(*freed(i, c - NJ))
                    transposes(xin, c, XT0)
                pe.wait_ge(*freed(i, WO[3] - NJ))
                out_projection(WO[3], 3)
                pe.wait_ge(y_done, NPAIR * i + (1 + NPAIR))
                for c in range(YT0, YT0 + 4):
                    pe.wait_ge(*freed(i, c - NJ))
                    transposes(y, c, YT0)
            for k in range(NJ):
                pe.wait_ge(j_free[k], each[k] * NB + before[k])
            for j in range(4):
                if j >= NJ:
                    pe.wait_ge(j_free[j % NJ], each[j % NJ] * NB + before[j % NJ] + 1)
                out_projection(j, j)

        @block.scalar
        def _(act):
            def high(dst, c, value):
                act.wait_ge(j_ready, value)
                act.activation(dst, bank_of(c)[:], ACT.Copy).then_inc(hi_done, 1)

            act.sem_inc(exp_done, 2)
            for c in range(4):
                high(xT[:, 0, 2 * c:2 * c + 2, :], c, c + 1)
            with act.Fori(0, NB) as i:
                def ready(c):
                    return NC * i + (FIRST + c + 1)
                for j in range(4):
                    act.wait_ge(j_ready, ready(V0 + j))
                    act.activation(v[:, 0, j // 2, bass.ts(j % 2, H // 2), 0:HD],
                                   bank_of(V0 + j)[:].rearrange("p (h d) -> p h d", d=HD),
                                   ACT.Copy, scale=1.0 / W_SCALE).then_inc(v_hi, 1)
                for s in range(NPAIR + 2):
                    if s < NPAIR:
                        act.wait_ge(qk_done, NPAIR * i + (s + 1))
                        act.wait_ge(j_ready, ready(QK0 + s))
                        act.activation(raw[:, s % 2].rearrange("p w n -> p (w n)"),
                                       bank_of(QK0 + s)[:], ACT.Copy,
                                       scale=1.0 / W_SCALE).then_inc(raw_done, 1)
                    if s >= 2:
                        for e in range(2):
                            act.wait_ge(pT_ready, H * i + (2 * (s - 2) + e + 1))
                            act.activation(probT[:, e, 0, :], ps_t[e][:, 0:3 * P], ACT.Copy) \
                                .then_inc(pT_hi, 1)
                    if 1 <= s <= NPAIR:
                        for e in range(2):
                            h = 2 * (s - 1) + e
                            act.wait_ge(max_done, 2 * H * i + (2 * h + 2))
                            act.activation(prob[:, h % 4, 0:P], ps_s[e][:, 0:P], ACT.Exp,
                                           bias=negmax[:, h % 4, 0:1])
                            act.activation(prob[:, h % 4, P:3 * P], ps_s[e][:, P:3 * P], ACT.Exp,
                                           bias=negmax[:, h % 4, 1:2]).then_inc(exp_done, 1)
                for c0, dst in ((XT0, xT), (YT0, yT)):
                    for k in range(4):
                        high(dst[:, 0, 2 * k:2 * k + 2, :], c0 + k, ready(c0 + k))

        @block.gpsimd
        def _(pool):
            def reciprocal_root(n):
                pool.wait_ge(ln_stat, 7 * n + 7)
                pool.tensor_tensor(rstd[:], rstd[:], minus_half[:], ALU.pow) \
                    .then_inc(ln_pow, 1)
            pool.memset(minus_half[:], -0.5).then_inc(zeroed, 1)
            pool.memset(v[:, 0, :, :, HD:HD + 1], 1.0).then_inc(zeroed, 1)
            pool.memset(v[:, 1, :, :, HD:HD + 1], 0.0).then_inc(zeroed, 1)
            pool.wait_ge(zeroed, 3)
            pool.wait_ge(consts_in, 32)
            reciprocal_root(0)
            with pool.Fori(0, NB) as i:
                for t in range(NPAIR):
                    pool.wait_ge(swapped[t % 2], 64 * (NPAIR // 2) * i + 64 * (t // 2 + 1))
                    pool.tensor_tensor(swp[:, t % 2], swp[:, t % 2], sin[:], ALU.mult) \
                        .then_inc(sin_done, 1)
                    if t == 5:
                        reciprocal_root(i + 1)

        @block.vector
        def _(dve):
            def norm_stats(n):
                dve.wait_ge(x_in, 16 * n + 16)
                for a in range(NT):
                    for b in range(2):
                        dve.bn_stats(stats[:, a, b, :], xin[:, a, bass.ts(b, BANK)]) \
                            .then_inc(ln_stat, 1)
                dve.wait_ge(ln_stat, 7 * n + 4)
                dve.memset(nothing[:], 0.0)
                for a in range(NT):
                    dve.bn_aggr(mv[:, a, :], stats[:, a]).then_inc(ln_stat, 1)
                dve.wait_ge(ln_stat, 7 * n + 6)
                dve.tensor_scalar(rstd[:], mv[:, :, 1], LN_EPS, None, ALU.add).then_inc(ln_stat, 1)

            def norm_apply(n):
                dve.wait_ge(ln_pow, n + 1)
                for a in range(NT):
                    dve.tensor_scalar(xin[:, a, :], xin[:, a, :], mv[:, a, 0:1], rstd[:, a:a + 1],
                                      ALU.subtract, ALU.mult).then_inc(ln_done, 1)

            def low(dst, hi, c, n, free):
                dve.wait_ge(hi_done, n)
                dve.tensor_tensor(dst, bank_of(c)[:].rearrange("p (a n) -> p a n", a=2), hi,
                                  ALU.subtract).then_inc(free, 1)

            def add_projection(c, j):
                n, half = j // 2, j % 2
                z = xres[:, n, bass.ts(half, BANK)]
                return dve.scalar_tensor_tensor(z, bank_of(c)[:], 1.0 / W_SCALE, z,
                                                ALU.mult, ALU.add)

            dve.sem_inc(qk_done, 2)
            dve.sem_inc(y_done, 1)
            dve.memset(yT[:], 0.0).then_inc(y_zero, 1)
            dve.wait_ge(consts_in, 32)
            norm_stats(0)
            norm_apply(0)
            for c in range(4):
                a = slice(2 * c, 2 * c + 2)
                low(xT[:, 1, a, :], xT[:, 0, a, :], c, c + 1, j_free[c % NJ])
            with dve.Fori(0, NB) as i:
                def ready(c):
                    return NC * i + (FIRST + c + 1)
                for j in range(4):
                    dve.wait_ge(v_hi, 4 * i + (j + 1))
                    heads = bass.ts(j % 2, H // 2)
                    dve.scalar_tensor_tensor(
                        v[:, 1, j // 2, heads, 0:HD],
                        bank_of(V0 + j)[:].rearrange("p (h d) -> p h d", d=HD), 1.0 / W_SCALE,
                        v[:, 0, j // 2, heads, 0:HD], ALU.mult, ALU.subtract) \
                        .then_inc(freed(i, V0 + j)[0], 1)
                for s in range(NPAIR + 2):
                    if s >= 2:
                        for e in range(2):
                            dve.wait_ge(pT_hi, H * i + (2 * (s - 2) + e + 1))
                            dve.tensor_tensor(probT[:, e, 1, :], ps_t[e][:, 0:3 * P],
                                              probT[:, e, 0, :], ALU.subtract).then_inc(pT_done, 1)
                    if s < NPAIR:
                        dve.wait_ge(raw_done, NPAIR * i + (s + 1))
                        dve.tensor_tensor(rot[:, s % 2], raw[:, s % 2], cos[:], ALU.mult) \
                            .then_inc(cos_done, 1)
                    if 1 <= s <= NPAIR:
                        for e in range(2):
                            h = 2 * (s - 1) + e
                            dve.wait_ge(s_ready, H * i + (h + 1))
                            for n, cols in enumerate((slice(0, P), slice(P, 3 * P))):
                                dve.tensor_reduce(negmax[:, h % 4, n:n + 1], ps_s[e][:, cols],
                                                  AX.X, ALU.max, negate=True).then_inc(max_done, 1)
                    if s >= 2:
                        t = s - 2
                        dve.wait_ge(o_ready, NPAIR * i + (t + 1))
                        dve.reciprocal(rinv[:], ps_o[:, :, :, HD]).then_inc(recip_done, 1)
                        if t == 0:
                            dve.wait_ge(j_ready, NC * i + FIRST)
                        dve.wait_ge(recip_done, NPAIR * i + (t + 1))
                        dve.tensor_tensor(
                            y[:, :, bass.ts(t, P)].rearrange("p n (e d) -> p e n d", e=2),
                            ps_o[:, :, :, 0:HD], rinv[:].unsqueeze(3).broadcast_to([P, 2, NT, HD]),
                            ALU.mult).then_inc(y_done, 1)
                    if s < NPAIR:
                        dve.wait_ge(sin_done, NPAIR * i + (s + 1))
                        dve.wait_ge(cos_done, NPAIR * i + (s + 1))
                        dve.tensor_tensor(rot[:, s % 2], rot[:, s % 2], swp[:, s % 2], ALU.add) \
                            .then_inc(rot_done, 1)
                        dve.wait_ge(rot_done, NPAIR * i + (s + 1))
                        dve.tensor_copy(qk[:, s % 2, 0], rot[:, s % 2]).then_inc(qk_hi, 1)
                        dve.wait_ge(qk_hi, NPAIR * i + (s + 1))
                        dve.tensor_tensor(qk[:, s % 2, 1], rot[:, s % 2], qk[:, s % 2, 0],
                                          ALU.subtract).then_inc(qk_done, 1)
                    else:
                        if s == NPAIR:
                            dve.wait_ge(res_in, 16 * i + 16)
                        c = WO[s - NPAIR]
                        dve.wait_ge(j_ready, ready(c))
                        add_projection(c, s - NPAIR).then_inc(freed(i, c)[0], 1)
                    if s == 4:
                        norm_stats(i + 1)
                    if s == 6:
                        norm_apply(i + 1)
                dve.wait_ge(j_ready, ready(WO[2]))
                add_projection(WO[2], 2).then_inc(freed(i, WO[2])[0], 1)
                for k in range(4):
                    a = slice(2 * k, 2 * k + 2)
                    low(xT[:, 1, a, :], xT[:, 0, a, :], XT0 + k, 8 * i + (4 + k + 1),
                        freed(i, XT0 + k)[0])
                dve.wait_ge(j_ready, ready(WO[3]))
                add_projection(WO[3], 3).then_inc(freed(i, WO[3])[0], 1)
                for k in range(4):
                    a = slice(2 * k, 2 * k + 2)
                    low(yT[:, 1, a, :], yT[:, 0, a, :], YT0 + k, 8 * i + (8 + k + 1),
                        freed(i, YT0 + k)[0])
            dve.wait_ge(res_in, 16 * NB + 16)
            for j in range(4):
                dve.wait_ge(j_ready, NC * NB + FIRST + j + 1)
                add_projection(j, j).then_inc(j_free[j % NJ], 1)


def second_half(nc, consts, banks, A, B, Wr, br, scratch, ctx, out):
    ident, ident_h, mask = consts
    ps_j, ps_s, ps_t, ps_ob = banks
    ps_o = ps_ob[:, 0:2 * NT * PVW].rearrange("p (e n d) -> p e n d", e=2, n=NT)
    st = ExitStack()

    def sb(name, shape, dt=F32):
        return st.enter_context(nc.sbuf_tensor(name, shape, dt))

    def sem(name):
        return st.enter_context(nc.semaphore(name))

    x_t = scratch.rearrange("b (n p) d -> b p n d", p=P)
    ctx_t = ctx.rearrange("b (n p) d -> b p n d", p=P)
    out_t = out.rearrange("b (n p) d -> b p n d", p=P)

    KT0, XT0, LG, H0, QT0, HT0, Y0, NC = 0, 4, 8, 9, 11, 15, 17, 21
    FIRST = 8
    RND = NC // NJ
    before = [len([c for c in range(FIRST) if c % NJ == k]) for k in range(NJ)]
    NHI = 14
    NSTEP = NPAIR + 2

    with st:
        aT = sb("aT", [P, 2, DT, ER], F16)
        bT = sb("bT", [P, 2, ERT, D], F16)
        rT = sb("rT", [P, 2, DT, E], F16)
        bias = sb("bias", [P, E])
        order = sb("order", [P, E])
        expert_weights(nc, ident, ps_j, aT, bT, rT, bias, order, A, B, Wr, br)

        kv = sb("kv", [P, NT, D])
        v = sb("v2", [P, 2, 2, NT, H, HD + 1], F16)
        kT = sb("kT", [P, 2, 2, DT, T], F16)
        qT = sb("qT", [P, 2, 2, DT, T], F16)
        x1 = sb("x1", [P, 2, NT, D])
        xn = sb("xn", [P, NT, D])
        x2 = sb("x2", [P, 2, NT, D])
        x3 = sb("x3", [P, NT, D])
        x3T = sb("x3T", [P, 2, DT, T], F16)
        hg = sb("hg", [P, NT, ER])
        hT = sb("hT", [P, 2, NT, ERT, P], F16)
        prob = sb("prob2", [P, 4, 3 * P])
        probT = sb("probT2", [P, 2, 2, 3 * P], F16)
        negmax = sb("negmax2", [P, 4, NT])
        rinv = sb("rinv2", [P, 2, NT])
        stats = sb("stats2", [P, NT, 2, 6])
        mv = sb("mv2", [P, NT, 2])
        rstd = sb("rstd2", [P, NT])
        nothing = sb("nothing2", [P, 1])
        minus_half = sb("minus_half2", [P, NT])
        logit = sb("logit", [P, NT, E])
        top = sb("top", [P, NT])
        gap = sb("gap", [P, NT, E])
        gexp = sb("gexp", [P, NT, E])
        rank = sb("rank", [P, NT, E])
        best = sb("best", [P, NT])
        total = sb("total", [P, NT])
        weight = sb("weight", [P, NT])
        onehot = sb("onehot", [P, NT, E])
        gate = sb("gate", [P, NT, E])

        ctx_in, x1_in, out_done = sem("ctx_in"), sem("x1_in"), sem("out_done")
        j_ready = sem("j_ready2")
        j_free = [sem(f"j_free2_{k}") for k in range(NJ)]
        hi_done = sem("hi_done2")
        v_hi = sem("v_hi2")
        v_done = sem("v_done2")
        s_ready = sem("s_ready2")
        max_done = sem("max_done2")
        exp_done = sem("exp_done2")
        pT_ready = sem("pT_ready2")
        pT_hi = sem("pT_hi2")
        pT_done = sem("pT_done2")
        o_ready = sem("o_ready2")
        recip_done = sem("recip_done2")
        y_done = sem("y_done2")
        x2_done = sem("x2_done")
        ln_stat = sem("ln_stat2")
        ln_pow = sem("ln_pow2")
        ln_done = sem("ln_done2")
        gating = sem("gating")
        gap_exp = sem("gap_exp")
        x2_zero = sem("x2_zero")
        zeroed = sem("zeroed2")
        block = st.enter_context(nc.Block())

        def bank_of(c):
            return ps_j[c % NJ]

        def in_round(i, b):
            return lambda n, k: 2 * n * i + (n * b + k)

        def after_rounds(n, k):
            return n * NB + k

        def free(at, c):
            return j_free[c % NJ], at(RND, before[c % NJ] + c // NJ)

        def used(at, c):
            return j_free[c % NJ], at(RND, before[c % NJ] + c // NJ + 1)

        def ready(at, c):
            return at(NC, FIRST + c + 1)

        @block.sync
        def _(sp):
            sp.sem_inc(out_done, 16)
            sp.dma_start(kv[:], ctx_t[0]).then_inc(ctx_in, 16)
            sp.dma_start(x1[:, 0], x_t[1]).then_inc(x1_in, 16)
            sp.wait_ge(j_ready, 4)
            sp.wait_ge(v_done, 2)
            sp.dma_start(kv[:], ctx_t[1]).then_inc(ctx_in, 16)
            with sp.Fori(0, NB // 2) as i:
                for b in range(2):
                    at = in_round(i, b)
                    sp.wait_ge(x2_done, at(NPAIR, 1))
                    sp.dma_start(x1[:, 1 - b], x_t[(2 * i + (b + 1)) % NB + 1]) \
                        .then_inc(x1_in, 16)
                    sp.wait_ge(v_done, at(2, 4))
                    sp.dma_start(kv[:], ctx_t[(2 * i + (b + 2)) % NB]).then_inc(ctx_in, 16)
                    sp.wait_ge(*used(at, Y0 + 3))
                    sp.dma_start(out_t[(2 * i + (b + NB - 1)) % NB], x2[:, 1 - b]) \
                        .then_inc(out_done, 16)
            sp.wait_ge(*used(after_rounds, LAST_Y + 3))
            sp.dma_start(out_t[NB - 1], x2[:, 1]).then_inc(out_done, 16)
            sp.wait_ge(ctx_in, 16 * (NB + 2))
            sp.wait_ge(out_done, 16 * (NB + 2))

        @block.tensor
        def _(pe):
            def transposes(src, c, k, at):
                pe.wait_ge(*free(at, c))
                for a in range(2):
                    for n in range(NT):
                        last = pe.transpose(bank_of(c)[:, bass.ts(a * NT + n, P)],
                                            src[:, n, bass.ts(2 * k + a, P)], ident[:])
                last.then_inc(j_ready, 1)

            def logits(c, at):
                pe.wait_ge(*free(at, c))
                for n in range(NT):
                    last = split_product(pe, bank_of(c)[:, bass.ts(n, E)],
                                         lambda i, a: x3T[:, i, a, bass.ts(n, P)],
                                         lambda i, a: rT[:, i, a, :], DT)
                last.then_inc(j_ready, 1)

            def hidden(c, n, at):
                pe.wait_ge(*free(at, c))
                split_product(pe, bank_of(c)[:], lambda i, a: x3T[:, i, a, bass.ts(n, P)],
                              lambda i, a: aT[:, i, a, :], DT).then_inc(j_ready, 1)

            def hidden_transposes(c, n, at):
                pe.wait_ge(*free(at, c))
                for a in range(ERT):
                    last = pe.transpose(bank_of(c)[:, bass.ts(a, P)], hg[:, n, bass.ts(a, P)],
                                        ident[:])
                last.then_inc(j_ready, 1)

            def expert_out(c, j, at):
                n, half = j // 2, j % 2
                pe.wait_ge(*free(at, c))
                split_product(pe, bank_of(c)[:], lambda i, a: hT[:, i, n, a, :],
                              lambda i, a: bT[:, i, a, bass.ts(half, BANK)], ERT) \
                    .then_inc(j_ready, 1)

            pe.wait_ge(zeroed, 5)
            pe.wait_ge(ctx_in, 16)
            for c in range(FIRST):
                if c == 4:
                    pe.wait_ge(ln_done, 2)
                if c >= NJ:
                    pe.wait_ge(j_free[c % NJ], c // NJ)
                for a in range(2):
                    for n in range(NT):
                        last = pe.transpose(bank_of(c)[:, bass.ts(a * NT + n, P)],
                                            (kv, xn)[c // 4][:, n, bass.ts(2 * (c % 4) + a, P)],
                                            ident[:])
                last.then_inc(j_ready, 1)
            with pe.Fori(0, NB // 2) as i:
                for b in range(2):
                    at = in_round(i, b)
                    for s in range(NSTEP):
                        if s == 0:
                            pe.wait_ge(ctx_in, at(16, 32))
                            for k in range(4):
                                transposes(kv, KT0 + k, k, at)
                        if s == 2:
                            pe.wait_ge(ln_done, at(4, 4))
                            for k in range(4):
                                transposes(x3, XT0 + k, k, at)
                        if s == 3:
                            pe.wait_ge(*used(at, XT0 + 3))
                            logits(LG, at)
                            hidden(H0, 0, at)
                        if s == 4:
                            hidden(H0 + 1, 1, at)
                        if s == 5:
                            pe.wait_ge(ln_done, at(4, 6))
                            for k in range(4):
                                transposes(xn, QT0 + k, k, at)
                        if s == 6:
                            for n in range(NT):
                                hidden_transposes(HT0 + n, n, at)
                        if s == 7:
                            pe.wait_ge(*used(at, HT0 + 1))
                        if s >= 7:
                            expert_out(Y0 + s - 7, s - 7, at)
                        if s == NSTEP - 1:
                            expert_out(Y0 + 3, 3, at)
                        if s >= 2:
                            for e in range(2):
                                h = 2 * (s - 2) + e
                                pe.wait_ge(exp_done, at(H, 2 + h + 1))
                                for k in range(3):
                                    last = pe.transpose(ps_t[e][:, bass.ts(k, P)],
                                                        prob[:, h % 4, bass.ts(k, P)], ident[:])
                                last.then_inc(pT_ready, 1)
                        if 1 <= s <= NPAIR:
                            t = s - 1
                            pe.wait_ge(exp_done, at(H, 2 * t + 2))
                            causal_scores(pe, ps_s, lambda i, r: qT[r, b, i, t],
                                          lambda i, r: kT[r, b, i, t], ident_h, mask, s_ready)
                        if s >= 2:
                            t = s - 2
                            if t == 0:
                                pe.wait_ge(v_done, at(2, 2))
                            pe.wait_ge(y_done, at(NPAIR, t + 1))
                            for e in range(2):
                                pe.wait_ge(pT_done, at(H, 2 * t + e + 1))
                                last = weights_times_values(
                                    pe, ps_o[:, e], lambda i, k: probT[:, e, i, bass.ts(k, P)],
                                    v[:, b], 2 * t + e)
                            last.then_inc(o_ready, 1)
            at = after_rounds
            pe.wait_ge(ln_done, at(4, 4))
            for k in range(4):
                transposes(x3, k, k, at)
            pe.wait_ge(*used(at, 3))
            logits(4, at)
            hidden(5, 0, at)
            hidden(6, 1, at)
            pe.wait_ge(*used(at, 6))
            for n in range(NT):
                hidden_transposes(7 + n, n, at)
            pe.wait_ge(*used(at, 8))
            for j in range(4):
                expert_out(LAST_Y + j, j, at)

        @block.scalar
        def _(act):
            def high(dst, c, at, scale=1.0):
                act.wait_ge(j_ready, ready(at, c))
                act.activation(dst, bank_of(c)[:], ACT.Copy, scale=scale).then_inc(hi_done, 1)

            def values(slot, wanted):
                act.wait_ge(ctx_in, wanted)
                for n in range(NT):
                    act.activation(v[:, slot, 0, n, :, 0:HD],
                                   kv[:, n].rearrange("p (h d) -> p h d", d=HD),
                                   ACT.Copy).then_inc(v_hi, 1)

            def gate_exp(wanted):
                act.wait_ge(gating, wanted)
                act.activation(gexp[:], gap[:], ACT.Exp).then_inc(gap_exp, 1)

            act.sem_inc(exp_done, 2)
            values(0, 16)
            for c in range(FIRST):
                act.wait_ge(j_ready, c + 1)
                k = c % 4
                act.activation((kT, qT)[c // 4][:, 0, 0, 2 * k:2 * k + 2, :], bank_of(c)[:],
                               ACT.Copy, scale=(1.0, HD ** -0.5)[c // 4]).then_inc(hi_done, 1)
            with act.Fori(0, NB // 2) as i:
                for b in range(2):
                    at = in_round(i, b)
                    for s in range(NSTEP):
                        if s == 0:
                            for k in range(4):
                                high(kT[:, 1 - b, 0, 2 * k:2 * k + 2, :], KT0 + k, at)
                            values(1 - b, at(16, 32))
                        if s == 2:
                            for k in range(4):
                                high(x3T[:, 0, 2 * k:2 * k + 2, :], XT0 + k, at)
                        if s == 4:
                            gate_exp(at(8, 2))
                        if s == 5:
                            for k in range(4):
                                high(qT[:, 1 - b, 0, 2 * k:2 * k + 2, :], QT0 + k, at, HD ** -0.5)
                        if s == 6:
                            for n in range(NT):
                                high(hT[:, 0, n], HT0 + n, at)
                        if s >= 2:
                            for e in range(2):
                                act.wait_ge(pT_ready, at(H, 2 * (s - 2) + e + 1))
                                act.activation(probT[:, e, 0, :], ps_t[e][:, 0:3 * P], ACT.Copy) \
                                    .then_inc(pT_hi, 1)
                        if 1 <= s <= NPAIR:
                            for e in range(2):
                                h = 2 * (s - 1) + e
                                act.wait_ge(max_done, at(2 * H, 2 * h + 2))
                                act.activation(prob[:, h % 4, 0:P], ps_s[e][:, 0:P], ACT.Exp,
                                               bias=negmax[:, h % 4, 0:1])
                                act.activation(prob[:, h % 4, P:3 * P], ps_s[e][:, P:3 * P],
                                               ACT.Exp, bias=negmax[:, h % 4, 1:2]) \
                                    .then_inc(exp_done, 1)
            at = after_rounds
            for k in range(4):
                high(x3T[:, 0, 2 * k:2 * k + 2, :], k, at)
            gate_exp(at(8, 2))
            for n in range(NT):
                high(hT[:, 0, n], 7 + n, at)

        @block.gpsimd
        def _(pool):
            def reciprocal_root(wanted):
                pool.wait_ge(ln_stat, wanted)
                pool.tensor_tensor(rstd[:], rstd[:], minus_half[:], ALU.pow) \
                    .then_inc(ln_pow, 1)

            def values(slot, wanted):
                for n in range(NT):
                    pool.wait_ge(v_hi, wanted[n])
                    pool.tensor_tensor(v[:, slot, 1, n, :, 0:HD],
                                       kv[:, n].rearrange("p (h d) -> p h d", d=HD),
                                       v[:, slot, 0, n, :, 0:HD], ALU.subtract) \
                        .then_inc(v_done, 1)

            pool.memset(minus_half[:], -0.5).then_inc(zeroed, 1)
            for b in range(2):
                pool.memset(v[:, b, 0, :, :, HD:HD + 1], 1.0).then_inc(zeroed, 1)
                pool.memset(v[:, b, 1, :, :, HD:HD + 1], 0.0).then_inc(zeroed, 1)
            pool.wait_ge(zeroed, 5)
            pool.sem_inc(x2_done, 1)
            values(0, (1, 2))
            reciprocal_root(7)
            with pool.Fori(0, NB // 2) as i:
                for b in range(2):
                    at = in_round(i, b)
                    reciprocal_root(at(14, 14))
                    values(1 - b, (at(2, 3), at(2, 4)))
                    pool.wait_ge(x1_in, at(16, 16))
                    for t in range(NPAIR):
                        pool.wait_ge(y_done, at(NPAIR, 1 + t + 1))
                        pair = bass.ts(t, P)
                        pool.tensor_tensor(x2[:, b, :, pair], x2[:, b, :, pair],
                                           x1[:, b, :, pair], ALU.add).then_inc(x2_done, 1)
                        if t == 0:
                            reciprocal_root(at(14, 21))
            reciprocal_root(after_rounds(14, 14))

        @block.vector
        def _(dve):
            def norm_stats(src, k):
                for a in range(NT):
                    for j in range(2):
                        dve.bn_stats(stats[:, a, j, :], src[:, a, bass.ts(j, BANK)]) \
                            .then_inc(ln_stat, 1)
                dve.wait_ge(ln_stat, k(4))
                dve.memset(nothing[:], 0.0)
                for a in range(NT):
                    dve.bn_aggr(mv[:, a, :], stats[:, a]).then_inc(ln_stat, 1)
                dve.wait_ge(ln_stat, k(6))
                dve.tensor_scalar(rstd[:], mv[:, :, 1], LN_EPS, None, ALU.add).then_inc(ln_stat, 1)

            def norm_apply(dst, src, wanted):
                dve.wait_ge(ln_pow, wanted)
                for a in range(NT):
                    dve.tensor_scalar(dst[:, a, :], src[:, a, :], mv[:, a, 0:1], rstd[:, a:a + 1],
                                      ALU.subtract, ALU.mult).then_inc(ln_done, 1)

            def low(dst, hi, c, k, at, scale=None):
                dve.wait_ge(hi_done, at(NHI, FIRST + k + 1))
                src = bank_of(c)[:].rearrange("p (a n) -> p a n", a=hi.shape[1])
                if scale is None:
                    last = dve.tensor_tensor(dst, src, hi, ALU.subtract)
                else:
                    last = dve.scalar_tensor_tensor(dst, src, scale, hi, ALU.mult, ALU.subtract)
                last.then_inc(j_free[c % NJ], 1)

            def add_expert_out(c, j, slot, at):
                n, half = j // 2, j % 2
                z = x2[:, slot, n, bass.ts(half, BANK)]
                dve.wait_ge(j_ready, ready(at, c))
                dve.scalar_tensor_tensor(z, bank_of(c)[:], 1.0 / (E_SCALE * R), z,
                                         ALU.mult, ALU.add).then_inc(j_free[c % NJ], 1)

            def gate_first(c, at):
                dve.wait_ge(j_ready, ready(at, c))
                dve.scalar_tensor_tensor(
                    logit[:], bank_of(c)[:, 0:NT * E].rearrange("p (n e) -> p n e", n=NT),
                    1.0 / E_SCALE, bias[:].unsqueeze(1).broadcast_to([P, NT, E]),
                    ALU.mult, ALU.add).then_inc(j_free[c % NJ], 1)
                dve.wait_ge(*used(at, c))
                dve.tensor_reduce(top[:], logit[:], AX.X, ALU.max).then_inc(gating, 1)
                dve.wait_ge(gating, at(8, 1))
                dve.tensor_tensor(gap[:], logit[:], top[:].unsqueeze(2).broadcast_to([P, NT, E]),
                                  ALU.subtract).then_inc(gating, 1)
                dve.wait_ge(gating, at(8, 2))
                dve.scalar_tensor_tensor(rank[:], gap[:], 0.0,
                                         order[:].unsqueeze(1).broadcast_to([P, NT, E]),
                                         ALU.is_equal, ALU.mult).then_inc(gating, 1)
                dve.wait_ge(gating, at(8, 3))
                dve.tensor_reduce(best[:], rank[:], AX.X, ALU.max).then_inc(gating, 1)

            def gate_second(n_exp, at):
                dve.wait_ge(gap_exp, n_exp)
                dve.tensor_reduce(total[:], gexp[:], AX.X, ALU.add).then_inc(gating, 1)
                dve.wait_ge(gating, at(8, 5))
                dve.reciprocal(weight[:], total[:]).then_inc(gating, 1)
                dve.tensor_tensor(onehot[:], rank[:], best[:].unsqueeze(2).broadcast_to([P, NT, E]),
                                  ALU.is_equal).then_inc(gating, 1)
                dve.wait_ge(gating, at(8, 7))
                dve.scalar_tensor_tensor(gate[:], onehot[:], 1.0 / E_SCALE,
                                         weight[:].unsqueeze(2).broadcast_to([P, NT, E]),
                                         ALU.mult, ALU.mult).then_inc(gating, 1)

            def gated(c, n, at):
                dve.wait_ge(j_ready, ready(at, c))
                if n == 0:
                    dve.wait_ge(gating, at(8, 8))
                dve.tensor_tensor(hg[:, n].rearrange("p (e r) -> p e r", e=E),
                                  bank_of(c)[:].rearrange("p (e r) -> p e r", e=E),
                                  gate[:, n].unsqueeze(2).broadcast_to([P, E, R]),
                                  ALU.mult).then_inc(j_free[c % NJ], 1)

            dve.sem_inc(y_done, 1)
            dve.memset(x2[:, 1], 0.0).then_inc(x2_zero, 1)
            dve.wait_ge(x1_in, 16)
            norm_stats(x1[:, 0], lambda k: k)
            norm_apply(xn, x1[:, 0], 1)
            for c in range(FIRST):
                k = slice(2 * (c % 4), 2 * (c % 4) + 2)
                dst = (kT, qT)[c // 4]
                dve.wait_ge(hi_done, c + 1)
                dve.scalar_tensor_tensor(dst[:, 0, 1, k, :],
                                         bank_of(c)[:].rearrange("p (a n) -> p a n", a=2),
                                         (1.0, HD ** -0.5)[c // 4], dst[:, 0, 0, k, :],
                                         ALU.mult, ALU.subtract).then_inc(j_free[c % NJ], 1)
            dve.wait_ge(x2_zero, 1)
            with dve.Fori(0, NB // 2) as i:
                for b in range(2):
                    at = in_round(i, b)
                    for s in range(NSTEP):
                        if s == 0:
                            dve.wait_ge(x2_done, at(NPAIR, 1))
                            norm_stats(x2[:, 1 - b], lambda k: at(14, 7 + k))
                            for k in range(4):
                                a = slice(2 * k, 2 * k + 2)
                                low(kT[:, 1 - b, 1, a, :], kT[:, 1 - b, 0, a, :], KT0 + k, k, at)
                        if s == 1:
                            norm_apply(x3, x2[:, 1 - b], at(2, 2))
                        if s == 2:
                            for k in range(4):
                                a = slice(2 * k, 2 * k + 2)
                                low(x3T[:, 1, a, :], x3T[:, 0, a, :], XT0 + k, 4 + k, at)
                        if s == 4:
                            gate_first(LG, at)
                        if s == 5:
                            for k in range(4):
                                a = slice(2 * k, 2 * k + 2)
                                low(qT[:, 1 - b, 1, a, :], qT[:, 1 - b, 0, a, :], QT0 + k, 8 + k,
                                    at, HD ** -0.5)
                        if s == 6:
                            for n in range(NT):
                                low(hT[:, 1, n], hT[:, 0, n], HT0 + n, 12 + n, at)
                        if s >= 8:
                            add_expert_out(Y0 + s - 8, s - 8, 1 - b, at)
                        if s >= 2:
                            for e in range(2):
                                dve.wait_ge(pT_hi, at(H, 2 * (s - 2) + e + 1))
                                dve.tensor_tensor(probT[:, e, 1, :], ps_t[e][:, 0:3 * P],
                                                  probT[:, e, 0, :], ALU.subtract) \
                                    .then_inc(pT_done, 1)
                        if 1 <= s <= NPAIR:
                            for e in range(2):
                                h = 2 * (s - 1) + e
                                dve.wait_ge(s_ready, at(H, h + 1))
                                for n, cols in enumerate((slice(0, P), slice(P, 3 * P))):
                                    dve.tensor_reduce(negmax[:, h % 4, n:n + 1], ps_s[e][:, cols],
                                                      AX.X, ALU.max, negate=True) \
                                        .then_inc(max_done, 1)
                        if s >= 2:
                            t = s - 2
                            dve.wait_ge(o_ready, at(NPAIR, t + 1))
                            dve.reciprocal(rinv[:], ps_o[:, :, :, HD]).then_inc(recip_done, 1)
                            if t == 0:
                                dve.wait_ge(out_done, at(16, 16))
                            dve.wait_ge(recip_done, at(NPAIR, t + 1))
                            dve.tensor_tensor(
                                x2[:, b, :, bass.ts(t, P)].rearrange("p n (e d) -> p e n d", e=2),
                                ps_o[:, :, :, 0:HD],
                                rinv[:].unsqueeze(3).broadcast_to([P, 2, NT, HD]),
                                ALU.mult).then_inc(y_done, 1)
                        if s == 2:
                            dve.wait_ge(x1_in, at(16, 32))
                            norm_stats(x1[:, 1 - b], lambda k: at(14, 14 + k))
                        if s == 3:
                            norm_apply(xn, x1[:, 1 - b], at(2, 3))
                        if s == 4:
                            gate_second(at(1, 1), at)
                            gated(H0, 0, at)
                            gated(H0 + 1, 1, at)
                    for j in (2, 3):
                        add_expert_out(Y0 + j, j, 1 - b, at)
            at = after_rounds
            dve.wait_ge(x2_done, at(NPAIR, 1))
            norm_stats(x2[:, 1], lambda k: at(14, 7 + k))
            norm_apply(x3, x2[:, 1], at(2, 2))
            for k in range(4):
                a = slice(2 * k, 2 * k + 2)
                low(x3T[:, 1, a, :], x3T[:, 0, a, :], k, k, at)
            gate_first(4, at)
            gate_second(at(1, 1), at)
            gated(5, 0, at)
            gated(6, 1, at)
            for n in range(NT):
                low(hT[:, 1, n], hT[:, 0, n], 7 + n, 4 + n, at)
            for j in range(4):
                add_expert_out(LAST_Y + j, j, 1, at)


LAST_Y = 9


def expert_weights(nc, ident, ps, aT, bT, rT, bias, order, A, B, Wr, br):
    with ExitStack() as st:
        a_in = st.enter_context(nc.sbuf_tensor("a_in", [P, ERT, D], F32))
        b_in = st.enter_context(nc.sbuf_tensor("b_in", [P, DT, ER], F32))
        r_in = st.enter_context(nc.sbuf_tensor("r_in", [E, D], F32))
        loaded = [st.enter_context(nc.semaphore(f"{n}_in_sem")) for n in ("a", "b", "r", "bias")]
        moved = st.enter_context(nc.semaphore("moved"))
        hi_kept = st.enter_context(nc.semaphore("hi_kept"))
        lo_kept = st.enter_context(nc.semaphore("lo_kept"))
        block = st.enter_context(nc.Block())

        def place(c):
            if c < 2 * ERT:
                k, j = c // 2, c % 2
                return [aT[:, i, 4 * j:4 * j + 4, bass.ts(k, P)] for i in range(2)]
            if c < 2 * ERT + DT:
                return [bT[:, i, :, bass.ts(c - 2 * ERT, P)] for i in range(2)]
            return [rT[:, i] for i in range(2)]

        def product(c):
            n = DT * E if c == 2 * ERT + DT else BANK
            return ps[c % NJ][:, 0:n].rearrange("p (a n) -> p a n", a=DT if n < BANK else 4)

        @block.sync
        def _(sp):
            sp.dma_start(a_in[:], A.rearrange("e r d -> (e r) d").rearrange("(k p) d -> p k d",
                                                                            p=P)) \
                .then_inc(loaded[0], 16)
            for k in range(DT):
                sp.dma_start(b_in[:, k].rearrange("p (e r) -> p e r", e=E),
                             B[:, k * P:k * P + P, :].rearrange("e p r -> p e r")) \
                    .then_inc(loaded[1], 16)
            sp.dma_start(r_in[:], Wr).then_inc(loaded[2], 16)
            sp.dma_start(bias[:], br.partition_broadcast(P)).then_inc(loaded[3], 16)
            sp.wait_ge(loaded[3], 16)

        @block.gpsimd
        def _(pool):
            for e in range(E):
                pool.memset(order[:, e:e + 1], float(E - e))

        @block.tensor
        def _(pe):
            for c in range(2 * ERT + DT + 1):
                if c >= NJ:
                    pe.wait_ge(lo_kept, c - NJ + 1)
                if c < 2 * ERT:
                    if c == 0:
                        pe.wait_ge(loaded[0], 16)
                    k, j = c // 2, c % 2
                    for a in range(4):
                        last = pe.transpose(ps[c % NJ][:, bass.ts(a, P)],
                                            a_in[:, k, bass.ts(4 * j + a, P)], ident[:])
                elif c < 2 * ERT + DT:
                    if c == 2 * ERT:
                        pe.wait_ge(loaded[1], 16 * DT)
                    for a in range(ERT):
                        last = pe.transpose(ps[c % NJ][:, bass.ts(a, P)],
                                            b_in[:, c - 2 * ERT, bass.ts(a, P)], ident[:])
                else:
                    pe.wait_ge(loaded[2], 16)
                    for a in range(DT):
                        last = pe.transpose(ps[c % NJ][:, bass.ts(a, E)],
                                            r_in[:, bass.ts(a, P)], ident[0:E, 0:E])
                last.then_inc(moved, 1)

        @block.scalar
        def _(act):
            for c in range(2 * ERT + DT + 1):
                act.wait_ge(moved, c + 1)
                act.activation(place(c)[0], product(c), ACT.Copy, scale=E_SCALE) \
                    .then_inc(hi_kept, 1)

        @block.vector
        def _(dve):
            for c in range(2 * ERT + DT + 1):
                dve.wait_ge(hi_kept, c + 1)
                dve.scalar_tensor_tensor(place(c)[1], product(c), E_SCALE, place(c)[0],
                                         ALU.mult, ALU.subtract).then_inc(lo_kept, 1)


def rope_tables():
    half = HD // 2
    freq = (np.float32(1) / np.float32(10000) ** (np.arange(half, dtype=np.float32)
                                                  / np.float32(half))).astype(np.float32)
    angle = np.outer(freq, np.arange(T, dtype=np.float32)).astype(np.float64)
    cos = np.tile(np.cos(angle), (4, 1))
    sin = np.concatenate([-np.sin(angle), np.sin(angle)] * 2)
    scales = np.array([HD ** -0.5, 1.0])
    return tuple((t[:, None, :] * scales[None, :, None]).astype(np.float32) for t in (cos, sin))


INPUTS = ("x", "ctx_2048", "L0_attn_w_q", "L0_attn_w_k", "L0_attn_w_v", "L0_attn_w_o",
          "L0_ffn_A", "L0_ffn_B", "L0_ffn_Wr", "L0_ffn_br")


def kernel(**inputs):
    import concourse.bacc as bacc
    from concourse.bass_utils import run_bass_kernel_spmd

    nc = bacc.Bacc("TRN2", target_bir_lowering=False, num_devices=1)
    cos, sin = rope_tables()
    arrays = {"in_" + name: np.ascontiguousarray(inputs[name]) for name in INPUTS}
    arrays["rope_cos"], arrays["rope_sin"] = cos, sin
    aps = [nc.dram_tensor(name, a.shape, F32, kind="ExternalInput").ap()
           for name, a in arrays.items()]
    out = nc.dram_tensor("out", (NB, T, D), F32, kind="ExternalOutput").ap()
    program(nc, *aps, out)
    result = run_bass_kernel_spmd(nc, [arrays], core_ids=[0])
    return result.results[0]["out"]
```

```python
from contextlib import ExitStack

import numpy as np

import concourse.bass as bass
from concourse import mybir

F32 = mybir.dt.float32
F16 = mybir.dt.float16
BF16 = mybir.dt.bfloat16
ALU = mybir.AluOpType
ACT = mybir.ActivationFunctionType
AX = mybir.AxisListType

P = 128
NB = 16
T = 256
NT = T // P
D = 1024
DT = D // P
H = 16
HD = D // H
NPAIR = H // 2
GROUP = 128
NG = D // GROUP
BANK = 512
NJ = 3
PVW = HD + 2
E = 8
R = 64
ER = E * R
ERT = ER // P
MASK = -1e30
W_SCALE = 256.0
E_SCALE = 64.0
LN_EPS = 1e-5
SCALE_EPS = 1e-8


def make_identity(pool, ident, ident_h, mask, done):
    pool.memset(ident[:], 0.0).then_inc(done, 1)
    pool.memset(mask[:], 0.0).then_inc(done, 1)
    pool.wait_ge(done, 2)
    pool.affine_select(out=ident[:], in_=ident[:], compare_op=ALU.not_equal, fill=1.0, base=0,
                       pattern=[[-1, P]], channel_multiplier=1).then_inc(done, 1)
    pool.affine_select(out=mask[:], in_=mask[:], compare_op=ALU.is_ge, fill=MASK, base=0,
                       pattern=[[-1, P]], channel_multiplier=1).then_inc(done, 1)
    pool.wait_ge(done, 3)
    pool.tensor_copy(ident_h[:], ident[:]).then_inc(done, 1)


IDENT_DONE = 5


def split_product(pe, out, lhs, rhs, n_tiles):
    for a in range(n_tiles):
        for k, (i, j) in enumerate(((0, 1), (1, 0), (0, 0))):
            last = pe.matmul(out, lhs(i, a), rhs(j, a), start=a == 0 and k == 0,
                             stop=a == n_tiles - 1 and k == 2)
    return last


def causal_scores(pe, banks, q, k, ident_h, mask, done):
    rows = [slice(HD * e, HD * e + HD) for e in range(2)]
    for i, j in ((0, 1), (1, 0), (0, 0)):
        for e in range(2):
            pe.matmul(banks[e][:, 0:P], q(i, rows[e])[:, 0:P], k(j, rows[e])[:, 0:P],
                      start=(i, j) == (0, 1), stop=False)
    for e in range(2):
        pe.matmul(banks[e][:, 0:P], ident_h[:], mask[:], start=False, stop=True)
    for i, j in ((0, 1), (1, 0), (0, 0)):
        for e in range(2):
            pe.matmul(banks[e][:, P:3 * P], q(i, rows[e])[:, P:T], k(j, rows[e]),
                      start=(i, j) == (0, 1), stop=False)
    for e in range(2):
        pe.matmul(banks[e][:, 2 * P:3 * P], ident_h[:], mask[:], start=False, stop=True) \
            .then_inc(done, 1)


def weights_times_values(pe, out, pT, v, h):
    for q, blocks in ((0, ((0, 0),)), (1, ((1, 0), (2, 1)))):
        for b, kt in blocks:
            for i, j in ((1, 0), (0, 1), (0, 0)):
                last = pe.matmul(out[:, q, 0:HD + 1], pT(i, b), v[:, j, kt, h, :],
                                 start=(i, j) == (1, 0) and kt == 0,
                                 stop=(i, j) == (0, 0) and b == blocks[-1][0])
    return last


def program(nc, x, ctx, w_q, w_k, w_v, w_o, A, B, Wr, br, rope_cos, rope_sin, out):
    scratch = nc.dram_tensor("after_self_attention", (NB + 1, T, D), F32, kind="Internal").ap()

    with ExitStack() as st:
        def sb(name, shape, dt=F32):
            return st.enter_context(nc.sbuf_tensor(name, shape, dt))

        ident = sb("ident", [P, P])
        ident_h = sb("ident_h", [P, P], BF16)
        mask = sb("mask", [P, P], BF16)
        ps_j = [st.enter_context(nc.psum_tensor(f"ps_j{k}", [P, BANK], F32)) for k in range(NJ)]
        ps_s = [st.enter_context(nc.psum_tensor(f"ps_s{k}", [P, BANK], F32)) for k in range(2)]
        ps_t = [st.enter_context(nc.psum_tensor(f"ps_t{k}", [P, BANK], F32)) for k in range(2)]
        ps_o = st.enter_context(nc.psum_tensor("ps_o", [P, BANK], F32))
        banks = (ps_j, ps_s, ps_t, ps_o)
        consts = (ident, ident_h, mask)
        with ExitStack() as st1:
            wT = [st1.enter_context(nc.sbuf_tensor(f"wT{m}", [P, 2, DT, D], F16))
                  for m in range(4)]
            early = [st1.enter_context(nc.sbuf_tensor(name, shape, F32)) for name, shape in
                     (("xin", [P, NT, D]), ("xres", [P, NT, D]), ("cos", [P, 2, T]),
                      ("sin", [P, 2, T]))]
            x_0 = x[0].rearrange("(n p) d -> p n d", p=P)
            weights(nc, consts, banks, wT, (w_q, w_k, w_v, w_o), early,
                    (x_0, x_0, rope_cos, rope_sin))
            self_attention(nc, consts, banks, wT, early, x, scratch)
        second_half(nc, consts, banks, A, B, Wr, br, scratch, ctx, out)


def weights(nc, consts, banks, wT, mats, early, early_from):
    ident, ident_h, mask = consts
    ps_j, ps_s, ps_t, ps_o = banks
    sets = [[ps_j[0], ps_j[1], ps_j[2], ps_s[0]], [ps_s[1], ps_t[0], ps_t[1], ps_o]]
    NS = 4

    with ExitStack() as st:
        def sb(name, shape, dt=F32):
            return st.enter_context(nc.sbuf_tensor(name, shape, dt))

        def sem(name):
            return st.enter_context(nc.semaphore(name))
        stage = sb("stage", [P, NS, D])
        above = sb("above", [P, NS, D], F16)
        below = sb("below", [P, NS, D], F16)
        diag = sb("diag", [P, NS, 2, NG, P], F16)
        ident_16 = sb("ident_16", [P, P], F16)
        asum = sb("asum", [P, NS, NG])
        scale = sb("scale", [P, NS, NG])
        scaleW = sb("scaleW", [P, NS, NG])
        high = sb("high", [P, NS, NG], F16)
        low = sb("low", [P, NS, NG], F16)
        thr = sb("thr", [P, NS, 2, NG])
        consts_done = sem("consts_done")
        w_in = [sem(f"w_in{p}") for p in range(NS)]
        early_in = sem("early_in")
        summed = sem("summed")
        scaled = sem("scaled")
        halved = sem("halved")
        low_done = sem("low_done")
        compared = sem("compared")
        signs = sem("signs")
        diag_lo = sem("diag_lo")
        diag_hi = sem("diag_hi")
        block_done = sem("block_done")
        kept = sem("kept")
        block = st.enter_context(nc.Block())

        @block.sync
        def _(sp):
            for m in range(4):
                rows = mats[m].rearrange("(k p r) i -> k p r i", p=NS, r=P)
                with sp.Fori(0, DT // NS) as k:
                    for p in range(NS):
                        n = NS * k + (DT * m + p)
                        sp.wait_ge(compared, 2 * n + 2)
                        sp.dma_start(stage[:, p, :], rows[k, p]).then_inc(w_in[p], 16)
            for to, source in zip(early, early_from):
                sp.dma_start(to[:], source).then_inc(early_in, 16)
            sp.wait_ge(early_in, 16 * len(early))

        @block.gpsimd
        def _(pool):
            make_identity(pool, ident, ident_h, mask, consts_done)
            pool.tensor_copy(ident_16[:], ident[:]).then_inc(consts_done, 1)
            pool.wait_ge(consts_done, IDENT_DONE + 1)
            for m in range(4):
                with pool.Fori(0, DT // NS) as k:
                    for u in range(NS):
                        n = NS * k + (DT * m + u)
                        pool.wait_ge(low_done, n + 1)
                        pool.tensor_tensor(
                            diag[:, u, 1], ident_16[:].unsqueeze(1).broadcast_to([P, NG, P]),
                            low[:, u, :].unsqueeze(2).broadcast_to([P, NG, P]), ALU.mult) \
                            .then_inc(diag_lo, 1)
                        pool.wait_ge(compared, 2 * n + 10)
                        pool.tensor_tensor(above[:, u, :], above[:, u, :], below[:, u, :],
                                           ALU.subtract).then_inc(signs, 1)

        @block.vector
        def _(dve):
            dve.sem_inc(compared, 2 * NS)
            for m in range(4):
                with dve.Fori(0, DT // NS) as k:
                    for u in range(NS):
                        n = NS * k + (DT * m + u)
                        w = stage[:, u, :].rearrange("p (g i) -> p g i", g=NG)
                        dve.wait_ge(w_in[u], 16 * k + (16 * (DT // NS) * m + 16))
                        dve.tensor_reduce(asum[:, u, :], w, AX.X, ALU.add,
                                          apply_absolute_value=True).then_inc(summed, 1)
                        dve.wait_ge(block_done, n + 1)
                        dve.wait_ge(summed, n + 1)
                        dve.tensor_scalar(scale[:, u, :], asum[:, u, :], 1.0 / GROUP, SCALE_EPS,
                                          ALU.mult, ALU.max).then_inc(scaled, 1)
                        dve.wait_ge(scaled, n + 1)
                        dve.tensor_scalar(thr[:, u, 0, :], scale[:, u, :], 0.5, None,
                                          ALU.mult).then_inc(halved, 1)
                        dve.tensor_scalar(thr[:, u, 1, :], scale[:, u, :], -0.5, None,
                                          ALU.mult).then_inc(halved, 1)
                        dve.tensor_scalar(scaleW[:, u, :], scale[:, u, :], W_SCALE, None,
                                          ALU.mult).then_inc(halved, 1)
                        dve.tensor_scalar(high[:, u, :], scale[:, u, :], W_SCALE, None,
                                          ALU.mult).then_inc(halved, 1)
                        dve.wait_ge(halved, 4 * n + 4)
                        dve.tensor_tensor(low[:, u, :], scaleW[:, u, :], high[:, u, :],
                                          ALU.subtract).then_inc(low_done, 1)
                        for j, (to, op) in enumerate(((above, ALU.is_gt), (below, ALU.is_lt))):
                            dve.tensor_tensor(
                                to[:, u, :].rearrange("p (g i) -> p g i", g=NG), w,
                                thr[:, u, j, :].unsqueeze(2).broadcast_to([P, NG, GROUP]),
                                op).then_inc(compared, 1)

        @block.scalar
        def _(act):
            def diagonals(u, n):
                act.wait_ge(halved, 4 * n + 3)
                for g in range(NG):
                    last = act.activation(diag[:, u, 0, g, :], ident[:], ACT.Copy,
                                          scale=scaleW[:, u, g:g + 1])
                last.then_inc(diag_hi, 1)

            def keep(to, u, k, n):
                act.wait_ge(block_done, n + (NS + 1))
                for half in range(2):
                    for j in range(2):
                        act.activation(to[:, half, 4 * j:4 * j + 4, bass.ts(NS * k + u, P)],
                                       sets[u % 2][2 * half + j][:].rearrange(
                                           "p (g o) -> p g o", g=4),
                                       ACT.Copy).then_inc(kept, 1)

            act.sem_inc(kept, 8)
            act.wait_ge(consts_done, IDENT_DONE)

            for m in range(4):
                with act.Fori(0, DT // NS) as k:
                    for u in range(NS + 1):
                        if u < NS:
                            diagonals(u, NS * k + (DT * m + u))
                        if u > 0:
                            keep(wT[m], u - 1, k, NS * k + (DT * m + u - 1))

        @block.tensor
        def _(pe):
            pe.sem_inc(block_done, NS)
            for m in range(4):
                with pe.Fori(0, DT // NS) as k:
                    for u in range(NS):
                        n, p = NS * k + (DT * m + u), u % 2
                        pe.wait_ge(signs, n + 1)
                        pe.wait_ge(diag_lo, n + 1)
                        pe.wait_ge(diag_hi, n + 1)
                        pe.wait_ge(kept, 4 * n + 4)
                        for half in range(2):
                            for g in range(NG):
                                last = pe.matmul(sets[p][2 * half + g // 4][:, bass.ts(g % 4, P)],
                                                 above[:, u, bass.ts(g, P)], diag[:, u, half, g, :],
                                                 start=True, stop=True)
                        last.then_inc(block_done, 1)


def self_attention(nc, consts, banks, wT, early, x, scratch):
    st = ExitStack()

    def sb(name, shape, dt=F32):
        return st.enter_context(nc.sbuf_tensor(name, shape, dt))
    ident, ident_h, mask = consts
    ps_j, ps_s, ps_t, ps_ob = banks
    ps_o = ps_ob[:, 0:2 * NT * PVW].rearrange("p (e n d) -> p e n d", e=2, n=NT)
    wqT, wkT, wvT, woT = wT
    xin, xres, cos, sin = early
    xT = sb("xT", [P, 2, DT, T], F16)
    y = sb("y", [P, NT, D])
    yT = sb("yT", [P, 2, DT, T], F16)
    v = sb("v", [P, 2, NT, H, HD + 1], F16)
    raw = sb("raw", [P, 2, 2, T])
    swp = sb("swp", [P, 2, 2, T])
    rot = sb("rot", [P, 2, 2, T])
    qk = sb("qk", [P, 2, 2, 2, T], F16)
    prob = sb("prob", [P, 4, 3 * P])
    probT = sb("probT", [P, 2, 2, 3 * P], F16)
    negmax = sb("negmax", [P, 4, NT])
    rinv = sb("rinv", [P, 2, NT])
    stats = sb("stats", [P, NT, 2, 6])
    mv = sb("mv", [P, NT, 2])
    rstd = sb("rstd", [P, NT])
    nothing = sb("nothing", [P, 1])
    minus_half = sb("minus_half", [P, NT])
    x_t = x.rearrange("b (n p) d -> b p n d", p=P)
    scr_t = scratch.rearrange("b (n p) d -> b p n d", p=P)

    QK, V, WO, XT, YT = (0, 4, *range(6, 12)), (1, 2, 3, 5), (12, 13, 14, 18), \
        (15, 16, 17, 19), (20, 21, 22, 23)
    NC = 24
    FIRST = 4

    def counted(k, upto):
        return len([c for c in range(upto) if c % NJ == k and c not in QK])
    each = [counted(k, NC) for k in range(NJ)]
    before = [len([c for c in range(FIRST) if c % NJ == k]) for k in range(NJ)]

    with st:
        def sem(name):
            return st.enter_context(nc.semaphore(name))
        x_in = sem("x_in")
        res_in = sem("res_in")
        x1_out = sem("x1_out")
        swapped = [sem(f"swapped{p}") for p in range(2)]
        j_ready = sem("j_ready")
        j_free = [sem(f"j_free{k}") for k in range(NJ)]
        raw_done = sem("raw_done")
        cos_done = sem("cos_done")
        sin_done = sem("sin_done")
        rot_done = sem("rot_done")
        qk_hi = sem("qk_hi")
        qk_done = sem("qk_done")
        s_ready = sem("s_ready")
        max_done = sem("max_done")
        exp_done = sem("exp_done")
        pT_ready = sem("pT_ready")
        pT_hi = sem("pT_hi")
        pT_done = sem("pT_done")
        hi_done = sem("hi_done")
        v_hi = sem("v_hi")
        o_ready = sem("o_ready")
        recip_done = sem("recip_done")
        y_done = sem("y_done")
        ln_stat = sem("ln_stat")
        ln_pow = sem("ln_pow")
        ln_done = sem("ln_done")
        y_zero = sem("y_zero")
        zeroed = sem("zeroed")
        block = st.enter_context(nc.Block())

        def bank_of(c):
            return ps_j[c % NJ]

        def freed(i, c):
            if c in QK:
                return raw_done, NPAIR * i + (QK.index(c) + 1)
            return j_free[c % NJ], each[c % NJ] * i + (before[c % NJ] + counted(c % NJ, c + 1))

        @block.sync
        def _(sp):
            sp.sem_inc(res_in, 16)
            with sp.Fori(0, NB) as i:
                sp.wait_ge(j_ready, NC * i + (FIRST + 1))
                sp.dma_start(xin[:], x_t[(i + 1) % NB]).then_inc(x_in, 16)
                for t in range(NPAIR):
                    p = t % 2
                    sp.wait_ge(raw_done, NPAIR * i + (t + 1))
                    sp.wait_ge(qk_done, NPAIR * i + (t + 1))
                    for a in range(4):
                        b = a ^ 1
                        sp.dma_start(swp[32 * a:32 * a + 32, p], raw[32 * b:32 * b + 32, p]) \
                            .then_inc(swapped[p], 16)
                sp.wait_ge(*freed(i, WO[3]))
                sp.dma_start(scr_t[i], xres[:]).then_inc(x1_out, 16)
                sp.wait_ge(x1_out, 16 * i + 16)
                sp.dma_start(xres[:], x_t[i]).then_inc(res_in, 16)
            sp.wait_ge(j_free[0], each[0] * NB + (before[0] + 2))
            sp.dma_start(scr_t[NB], xres[:]).then_inc(x1_out, 16)
            sp.wait_ge(x1_out, 16 * NB + 16)

        @block.tensor
        def _(pe):
            def transposes(src, c, k):
                for a in range(2):
                    for n in range(NT):
                        last = pe.transpose(bank_of(c)[:, bass.ts(a * NT + n, P)],
                                            src[:, n, bass.ts(2 * k + a, P)], ident[:])
                last.then_inc(j_ready, 1)

            def out_projection(c, j):
                n, half = j // 2, j % 2
                split_product(pe, bank_of(c)[:], lambda i, a: yT[:, i, a, bass.ts(n, P)],
                              lambda i, a: woT[:, i, a, bass.ts(half, BANK)], DT) \
                    .then_inc(j_ready, 1)

            pe.wait_ge(zeroed, 3)
            pe.wait_ge(y_zero, 1)
            pe.wait_ge(ln_done, 2)
            for c in range(FIRST):
                if c >= NJ:
                    pe.wait_ge(j_free[c % NJ], 1)
                transposes(xin, c, c)
            with pe.Fori(0, NB) as i:
                def last_read(k):
                    pe.wait_ge(j_free[k], each[k] * i + before[k])

                def values(j):
                    c = V[j]
                    if c >= NJ:
                        pe.wait_ge(*freed(i, c - NJ))
                    else:
                        last_read(c)
                    split_product(pe, bank_of(c)[:], lambda i, a: xT[:, i, a, bass.ts(j // 2, P)],
                                  lambda i, a: wvT[:, i, a, bass.ts(j % 2, BANK)], DT) \
                        .then_inc(j_ready, 1)

                for s in range(NPAIR + 2):
                    if s == 1:
                        for j in range(3):
                            values(j)
                    if s < NPAIR:
                        c = QK[s]
                        if c >= NJ:
                            pe.wait_ge(*freed(i, c - NJ))
                        else:
                            last_read(c)
                        for w, m in enumerate((wqT, wkT)):
                            last = split_product(pe, bank_of(c)[:, bass.ts(w, T)],
                                                 lambda i, a: m[:, i, a, bass.ts(s, P)],
                                                 lambda i, a: xT[:, i, a, :], DT)
                        last.then_inc(j_ready, 1)
                    else:
                        c = WO[s - NPAIR]
                        pe.wait_ge(*freed(i, c - NJ))
                        out_projection(c, s - NPAIR)
                    if s == 1:
                        values(3)
                    if s >= 2:
                        for e in range(2):
                            h = 2 * (s - 2) + e
                            pe.wait_ge(exp_done, H * i + (2 + h + 1))
                            for k in range(3):
                                last = pe.transpose(ps_t[e][:, bass.ts(k, P)],
                                                    prob[:, h % 4, bass.ts(k, P)], ident[:])
                            last.then_inc(pT_ready, 1)
                    if 1 <= s <= NPAIR:
                        t = s - 1
                        pe.wait_ge(qk_done, NPAIR * i + (2 + t + 1))
                        pe.wait_ge(exp_done, H * i + (2 * t + 2))
                        causal_scores(pe, ps_s, lambda i, r: qk[r, t % 2, i, 0],
                                      lambda i, r: qk[r, t % 2, i, 1], ident_h, mask, s_ready)
                    if s == NPAIR + 1:
                        pe.wait_ge(*freed(i, WO[2] - NJ))
                        out_projection(WO[2], 2)
                    if s >= 2:
                        t = s - 2
                        pe.wait_ge(y_done, NPAIR * i + (t + 1))
                        for e in range(2):
                            pe.wait_ge(pT_done, H * i + (2 * t + e + 1))
                            last = weights_times_values(
                                pe, ps_o[:, e], lambda i, b: probT[:, e, i, bass.ts(b, P)],
                                v, 2 * t + e)
                        last.then_inc(o_ready, 1)
                pe.wait_ge(ln_done, 2 * i + 4)
                for k, c in enumerate(XT):
                    if k == 3:
                        pe.wait_ge(*freed(i, WO[3] - NJ))
                        out_projection(WO[3], 3)
                    pe.wait_ge(*freed(i, c - NJ))
                    transposes(xin, c, k)
                pe.wait_ge(y_done, NPAIR * i + (1 + NPAIR))
                for k, c in enumerate(YT):
                    pe.wait_ge(*freed(i, c - NJ))
                    transposes(y, c, k)
            for k in range(NJ):
                pe.wait_ge(j_free[k], each[k] * NB + before[k])
            for j in range(4):
                if j >= NJ:
                    pe.wait_ge(j_free[j % NJ], each[j % NJ] * NB + before[j % NJ] + 1)
                out_projection(j, j)

        @block.scalar
        def _(act):
            def high(dst, c, value):
                act.wait_ge(j_ready, value)
                act.activation(dst, bank_of(c)[:], ACT.Copy).then_inc(hi_done, 1)

            act.sem_inc(exp_done, 2)
            for c in range(4):
                high(xT[:, 0, 2 * c:2 * c + 2, :], c, c + 1)
            with act.Fori(0, NB) as i:
                def ready(c):
                    return NC * i + (FIRST + c + 1)
                def high_values(j):
                    act.wait_ge(j_ready, ready(V[j]))
                    act.activation(v[:, 0, j // 2, bass.ts(j % 2, H // 2), 0:HD],
                                   bank_of(V[j])[:].rearrange("p (h d) -> p h d", d=HD),
                                   ACT.Copy, scale=1.0 / W_SCALE).then_inc(v_hi, 1)

                for s in range(NPAIR + 2):
                    if s == 1:
                        for j in range(3):
                            high_values(j)
                    if s < NPAIR:
                        act.wait_ge(qk_done, NPAIR * i + (s + 1))
                        act.wait_ge(j_ready, ready(QK[s]))
                        act.activation(raw[:, s % 2].rearrange("p w n -> p (w n)"),
                                       bank_of(QK[s])[:], ACT.Copy,
                                       scale=1.0 / W_SCALE).then_inc(raw_done, 1)
                    if s == 1:
                        high_values(3)
                    if s >= 2:
                        for e in range(2):
                            act.wait_ge(pT_ready, H * i + (2 * (s - 2) + e + 1))
                            act.activation(probT[:, e, 0, :], ps_t[e][:, 0:3 * P], ACT.Copy) \
                                .then_inc(pT_hi, 1)
                    if 1 <= s <= NPAIR:
                        for e in range(2):
                            h = 2 * (s - 1) + e
                            act.wait_ge(max_done, 2 * H * i + (2 * h + 2))
                            act.activation(prob[:, h % 4, 0:P], ps_s[e][:, 0:P], ACT.Exp,
                                           bias=negmax[:, h % 4, 0:1])
                            act.activation(prob[:, h % 4, P:3 * P], ps_s[e][:, P:3 * P], ACT.Exp,
                                           bias=negmax[:, h % 4, 1:2]).then_inc(exp_done, 1)
                for cs, dst in ((XT, xT), (YT, yT)):
                    for k, c in enumerate(cs):
                        high(dst[:, 0, 2 * k:2 * k + 2, :], c, ready(c))

        @block.gpsimd
        def _(pool):
            def reciprocal_root(n):
                pool.wait_ge(ln_stat, 7 * n + 7)
                pool.tensor_tensor(rstd[:], rstd[:], minus_half[:], ALU.pow) \
                    .then_inc(ln_pow, 1)
            pool.memset(minus_half[:], -0.5).then_inc(zeroed, 1)
            pool.memset(v[:, 0, :, :, HD:HD + 1], 1.0).then_inc(zeroed, 1)
            pool.memset(v[:, 1, :, :, HD:HD + 1], 0.0).then_inc(zeroed, 1)
            pool.wait_ge(zeroed, 3)
            reciprocal_root(0)
            with pool.Fori(0, NB) as i:
                for t in range(NPAIR):
                    pool.wait_ge(swapped[t % 2], 64 * (NPAIR // 2) * i + 64 * (t // 2 + 1))
                    pool.tensor_tensor(swp[:, t % 2], swp[:, t % 2], sin[:], ALU.mult) \
                        .then_inc(sin_done, 1)
                    if t == 4:
                        reciprocal_root(i + 1)

        @block.vector
        def _(dve):
            def norm_stats(n):
                for a in range(NT):
                    tile_stats(a)
                norm_sums(n)

            def tile_stats(a):
                for b in range(2):
                    dve.bn_stats(stats[:, a, b, :], xin[:, a, bass.ts(b, BANK)]) \
                        .then_inc(ln_stat, 1)

            def norm_sums(n):
                dve.wait_ge(ln_stat, 7 * n + 4)
                dve.memset(nothing[:], 0.0)
                for a in range(NT):
                    dve.bn_aggr(mv[:, a, :], stats[:, a]).then_inc(ln_stat, 1)
                dve.wait_ge(ln_stat, 7 * n + 6)
                dve.tensor_scalar(rstd[:], mv[:, :, 1], LN_EPS, None, ALU.add).then_inc(ln_stat, 1)

            def norm_apply(n, tiles=range(NT)):
                dve.wait_ge(ln_pow, n + 1)
                for a in tiles:
                    dve.tensor_scalar(xin[:, a, :], xin[:, a, :], mv[:, a, 0:1], rstd[:, a:a + 1],
                                      ALU.subtract, ALU.mult).then_inc(ln_done, 1)

            def low(dst, hi, c, n, free):
                dve.wait_ge(hi_done, n)
                dve.tensor_tensor(dst, bank_of(c)[:].rearrange("p (a n) -> p a n", a=2), hi,
                                  ALU.subtract).then_inc(free, 1)

            def add_projection(c, j):
                n, half = j // 2, j % 2
                z = xres[:, n, bass.ts(half, BANK)]
                return dve.scalar_tensor_tensor(z, bank_of(c)[:], 1.0 / W_SCALE, z,
                                                ALU.mult, ALU.add)

            dve.sem_inc(qk_done, 2)
            dve.sem_inc(y_done, 1)
            dve.memset(yT[:], 0.0).then_inc(y_zero, 1)
            norm_stats(0)
            norm_apply(0)
            for c in range(4):
                a = slice(2 * c, 2 * c + 2)
                low(xT[:, 1, a, :], xT[:, 0, a, :], c, c + 1, j_free[c % NJ])
            with dve.Fori(0, NB) as i:
                def ready(c):
                    return NC * i + (FIRST + c + 1)
                def low_values(j):
                    dve.wait_ge(v_hi, 4 * i + (j + 1))
                    heads = bass.ts(j % 2, H // 2)
                    dve.scalar_tensor_tensor(
                        v[:, 1, j // 2, heads, 0:HD],
                        bank_of(V[j])[:].rearrange("p (h d) -> p h d", d=HD),
                        1.0 / W_SCALE, v[:, 0, j // 2, heads, 0:HD],
                        ALU.mult, ALU.subtract).then_inc(freed(i, V[j])[0], 1)

                for s in range(NPAIR + 2):
                    if s == 1:
                        for j in range(3):
                            low_values(j)
                    if s >= NPAIR:
                        if s == NPAIR:
                            dve.wait_ge(res_in, 16 * i + 16)
                        c = WO[s - NPAIR]
                        dve.wait_ge(j_ready, ready(c))
                        add_projection(c, s - NPAIR).then_inc(freed(i, c)[0], 1)
                    if s >= 2:
                        for e in range(2):
                            dve.wait_ge(pT_hi, H * i + (2 * (s - 2) + e + 1))
                            dve.tensor_tensor(probT[:, e, 1, :], ps_t[e][:, 0:3 * P],
                                              probT[:, e, 0, :], ALU.subtract).then_inc(pT_done, 1)
                    if s < NPAIR:
                        dve.wait_ge(raw_done, NPAIR * i + (s + 1))
                        dve.tensor_tensor(rot[:, s % 2], raw[:, s % 2], cos[:], ALU.mult) \
                            .then_inc(cos_done, 1)
                    if s == 1:
                        low_values(3)
                    if 1 <= s <= NPAIR:
                        for e in range(2):
                            h = 2 * (s - 1) + e
                            dve.wait_ge(s_ready, H * i + (h + 1))
                            for n, cols in enumerate((slice(0, P), slice(P, 3 * P))):
                                dve.tensor_reduce(negmax[:, h % 4, n:n + 1], ps_s[e][:, cols],
                                                  AX.X, ALU.max, negate=True).then_inc(max_done, 1)
                    if s >= 2:
                        t = s - 2
                        dve.wait_ge(o_ready, NPAIR * i + (t + 1))
                        dve.reciprocal(rinv[:], ps_o[:, :, :, HD]).then_inc(recip_done, 1)
                        if t == 0:
                            dve.wait_ge(j_ready, NC * i + FIRST)
                        dve.wait_ge(recip_done, NPAIR * i + (t + 1))
                        dve.tensor_tensor(
                            y[:, :, bass.ts(t, P)].rearrange("p n (e d) -> p e n d", e=2),
                            ps_o[:, :, :, 0:HD], rinv[:].unsqueeze(3).broadcast_to([P, 2, NT, HD]),
                            ALU.mult).then_inc(y_done, 1)
                    if s == 3:
                        dve.wait_ge(x_in, 16 * i + 16)
                        tile_stats(0)
                    if s == 4:
                        tile_stats(1)
                        norm_sums(i + 1)
                    if s == 5:
                        norm_apply(i + 1, (0,))
                    if s == 6:
                        norm_apply(i + 1, (1,))
                    if s < NPAIR:
                        dve.wait_ge(sin_done, NPAIR * i + (s + 1))
                        dve.wait_ge(cos_done, NPAIR * i + (s + 1))
                        dve.tensor_tensor(rot[:, s % 2], rot[:, s % 2], swp[:, s % 2], ALU.add) \
                            .then_inc(rot_done, 1)
                        dve.wait_ge(rot_done, NPAIR * i + (s + 1))
                        dve.tensor_copy(qk[:, s % 2, 0], rot[:, s % 2]).then_inc(qk_hi, 1)
                        dve.wait_ge(qk_hi, NPAIR * i + (s + 1))
                        dve.tensor_tensor(qk[:, s % 2, 1], rot[:, s % 2], qk[:, s % 2, 0],
                                          ALU.subtract).then_inc(qk_done, 1)
                dve.wait_ge(j_ready, ready(WO[2]))
                add_projection(WO[2], 2).then_inc(freed(i, WO[2])[0], 1)
                for k, c in enumerate(XT):
                    if k == 3:
                        dve.wait_ge(j_ready, ready(WO[3]))
                        add_projection(WO[3], 3).then_inc(freed(i, WO[3])[0], 1)
                    a = slice(2 * k, 2 * k + 2)
                    low(xT[:, 1, a, :], xT[:, 0, a, :], c, 8 * i + (4 + k + 1), freed(i, c)[0])
                for k, c in enumerate(YT):
                    a = slice(2 * k, 2 * k + 2)
                    low(yT[:, 1, a, :], yT[:, 0, a, :], c, 8 * i + (8 + k + 1), freed(i, c)[0])
            dve.wait_ge(res_in, 16 * NB + 16)
            for j in range(4):
                dve.wait_ge(j_ready, NC * NB + FIRST + j + 1)
                add_projection(j, j).then_inc(j_free[j % NJ], 1)


def second_half(nc, consts, banks, A, B, Wr, br, scratch, ctx, out):
    ident, ident_h, mask = consts
    ps_j, ps_s, ps_t, ps_ob = banks
    ps_o = ps_ob[:, 0:2 * NT * PVW].rearrange("p (e n d) -> p e n d", e=2, n=NT)
    st = ExitStack()

    def sb(name, shape, dt=F32):
        return st.enter_context(nc.sbuf_tensor(name, shape, dt))

    def sem(name):
        return st.enter_context(nc.semaphore(name))

    x_t = scratch.rearrange("b (n p) d -> b p n d", p=P)
    ctx_t = ctx.rearrange("b (n p) d -> b p n d", p=P)
    out_t = out.rearrange("b (n p) d -> b p n d", p=P)

    QT0, XT0, LG, H0, HT0, KT0, Y0, NC = 0, 4, 8, 9, 11, 13, 17, 21
    FIRST = 8
    RND = NC // NJ
    before = [len([c for c in range(FIRST) if c % NJ == k]) for k in range(NJ)]
    NHI = 14
    NSTEP = NPAIR + 1

    with st:
        aT = sb("aT", [P, 2, DT, ER], F16)
        bT = sb("bT", [P, 2, ERT, D], F16)
        rT = sb("rT", [P, 2, DT, E], F16)
        bias = sb("bias", [P, E])
        order = sb("order", [P, E])
        kv = sb("kv", [P, NT, D])
        v = sb("v2", [P, 2, 2, NT, H, HD + 1], F16)
        kT = sb("kT", [P, 2, 2, DT, T], F16)
        qT = sb("qT", [P, 2, 2, DT, T], F16)
        x1 = sb("x1", [P, 2, NT, D])
        xn = sb("xn", [P, NT, D])
        expert_weights(nc, ident, ps_j, aT, bT, rT, bias, order, A, B, Wr, br,
                       ((kv[:], ctx_t[0]), (xn[:], x_t[1]), (x1[:, 0], x_t[1])))
        x2 = sb("x2", [P, 2, NT, D])
        x3 = sb("x3", [P, NT, D])
        x3T = sb("x3T", [P, 2, DT, T], F16)
        hg = sb("hg", [P, NT, ER])
        hT = sb("hT", [P, 2, NT, ERT, P], F16)
        prob = sb("prob2", [P, 4, 3 * P])
        probT = sb("probT2", [P, 2, 2, 3 * P], F16)
        negmax = sb("negmax2", [P, 4, NT])
        rinv = sb("rinv2", [P, 2, NT])
        stats = sb("stats2", [P, NT, 2, 6])
        stats_x2 = sb("stats_x2", [P, NT, 2, 6])
        mv = sb("mv2", [P, NT, 2])
        rstd = sb("rstd2", [P, NT])
        nothing = sb("nothing2", [P, 1])
        minus_mean = sb("minus_mean", [P, NT])
        offset = sb("offset", [P, NT])
        minus_half = sb("minus_half2", [P, NT])
        logit = sb("logit", [P, NT, E])
        top = sb("top", [P, NT])
        gap = sb("gap", [P, NT, E])
        gexp = sb("gexp", [P, NT, E])
        rank = sb("rank", [P, NT, E])
        best = sb("best", [P, NT])
        total = sb("total", [P, NT])
        weight = sb("weight", [P, NT])
        onehot = sb("onehot", [P, NT, E])
        gate = sb("gate", [P, NT, E])

        ctx_in, x1_in, out_done = sem("ctx_in"), sem("x1_in"), sem("out_done")
        xn_in = sem("xn_in")
        j_ready = sem("j_ready2")
        j_free = [sem(f"j_free2_{k}") for k in range(NJ)]
        hi_done = sem("hi_done2")
        v_hi = sem("v_hi2")
        v_done = sem("v_done2")
        s_ready = sem("s_ready2")
        max_done = sem("max_done2")
        exp_done = sem("exp_done2")
        pT_ready = sem("pT_ready2")
        pT_hi = sem("pT_hi2")
        pT_done = sem("pT_done2")
        o_ready = sem("o_ready2")
        recip_done = sem("recip_done2")
        y_done = sem("y_done2")
        x2_done = sem("x2_done")
        ln_stat = sem("ln_stat2")
        ln_pow = sem("ln_pow2")
        ln_done = sem("ln_done2")
        gating = sem("gating")
        gap_exp = sem("gap_exp")
        x2_zero = sem("x2_zero")
        zeroed = sem("zeroed2")
        block = st.enter_context(nc.Block())

        def bank_of(c):
            return ps_j[c % NJ]

        def in_round(i, b):
            return lambda n, k: 2 * n * i + (n * b + k)

        def after_rounds(n, k):
            return n * NB + k

        def free(at, c):
            return j_free[c % NJ], at(RND, before[c % NJ] + c // NJ)

        def used(at, c):
            return j_free[c % NJ], at(RND, before[c % NJ] + c // NJ + 1)

        def ready(at, c):
            return at(NC, FIRST + c + 1)

        @block.sync
        def _(sp):
            sp.sem_inc(out_done, 16)
            sp.sem_inc(ctx_in, 16)
            sp.sem_inc(x1_in, 16)
            sp.sem_inc(xn_in, 16)
            sp.wait_ge(v_done, 2)
            sp.dma_start(kv[:], ctx_t[1]).then_inc(ctx_in, 16)
            sp.wait_ge(j_ready, FIRST)
            sp.dma_start(xn[:], x_t[2]).then_inc(xn_in, 16)
            with sp.Fori(0, NB // 2) as i:
                for b in range(2):
                    at = in_round(i, b)
                    sp.wait_ge(x2_done, at(NPAIR, 1))
                    sp.dma_start(x1[:, 1 - b], x_t[(2 * i + (b + 1)) % NB + 1]) \
                        .then_inc(x1_in, 16)
                    sp.wait_ge(j_ready, ready(at, QT0 + 3))
                    sp.dma_start(xn[:], x_t[(2 * i + (b + 2)) % NB + 1]).then_inc(xn_in, 16)
                    sp.wait_ge(j_ready, ready(at, KT0 + 3))
                    sp.dma_start(kv[:], ctx_t[(2 * i + (b + 2)) % NB]).then_inc(ctx_in, 16)
                    sp.wait_ge(*used(at, Y0 + 3))
                    sp.dma_start(out_t[(2 * i + (b + NB - 1)) % NB], x2[:, 1 - b]) \
                        .then_inc(out_done, 16)
            sp.wait_ge(*used(after_rounds, LAST_Y + 3))
            sp.dma_start(out_t[NB - 1], x2[:, 1]).then_inc(out_done, 16)
            sp.wait_ge(ctx_in, 16 * (NB + 2))
            sp.wait_ge(out_done, 16 * (NB + 2))

        @block.tensor
        def _(pe):
            def transposes(src, c, k, at):
                pe.wait_ge(*free(at, c))
                for a in range(2):
                    for n in range(NT):
                        last = pe.transpose(bank_of(c)[:, bass.ts(a * NT + n, P)],
                                            src[:, n, bass.ts(2 * k + a, P)], ident[:])
                last.then_inc(j_ready, 1)

            def logits(c, at):
                pe.wait_ge(*free(at, c))
                for n in range(NT):
                    last = split_product(pe, bank_of(c)[:, bass.ts(n, E)],
                                         lambda i, a: x3T[:, i, a, bass.ts(n, P)],
                                         lambda i, a: rT[:, i, a, :], DT)
                last.then_inc(j_ready, 1)

            def hidden(c, n, at):
                pe.wait_ge(*free(at, c))
                split_product(pe, bank_of(c)[:], lambda i, a: x3T[:, i, a, bass.ts(n, P)],
                              lambda i, a: aT[:, i, a, :], DT).then_inc(j_ready, 1)

            def hidden_transposes(c, n, at):
                pe.wait_ge(*free(at, c))
                for a in range(ERT):
                    last = pe.transpose(bank_of(c)[:, bass.ts(a, P)], hg[:, n, bass.ts(a, P)],
                                        ident[:])
                last.then_inc(j_ready, 1)

            def expert_out(c, j, at):
                n, half = j // 2, j % 2
                pe.wait_ge(*free(at, c))
                split_product(pe, bank_of(c)[:], lambda i, a: hT[:, i, n, a, :],
                              lambda i, a: bT[:, i, a, bass.ts(half, BANK)], ERT) \
                    .then_inc(j_ready, 1)

            pe.wait_ge(zeroed, 5)
            pe.wait_ge(ctx_in, 16)
            for c in range(FIRST):
                if c == 4:
                    pe.wait_ge(ln_done, 2)
                if c >= NJ:
                    pe.wait_ge(j_free[c % NJ], c // NJ)
                for a in range(2):
                    for n in range(NT):
                        last = pe.transpose(bank_of(c)[:, bass.ts(a * NT + n, P)],
                                            (kv, xn)[c // 4][:, n, bass.ts(2 * (c % 4) + a, P)],
                                            ident[:])
                last.then_inc(j_ready, 1)
            with pe.Fori(0, NB // 2) as i:
                for b in range(2):
                    at = in_round(i, b)
                    for s in range(NSTEP):
                        if s == 0:
                            for c in range(NJ):
                                pe.wait_ge(*free(at, c))
                        if s < NPAIR:
                            pe.wait_ge(exp_done, at(H, 2 * s + 2))
                            causal_scores(pe, ps_s, lambda i, r: qT[r, b, i, s],
                                          lambda i, r: kT[r, b, i, s], ident_h, mask, s_ready)
                        if s >= 1:
                            for e in range(2):
                                h = 2 * (s - 1) + e
                                pe.wait_ge(exp_done, at(H, 2 + h + 1))
                                for k in range(3):
                                    last = pe.transpose(ps_t[e][:, bass.ts(k, P)],
                                                        prob[:, h % 4, bass.ts(k, P)], ident[:])
                                last.then_inc(pT_ready, 1)
                        if s == 0:
                            pe.wait_ge(ln_done, at(4, 4))
                        if s <= 1:
                            for k in (2 * s, 2 * s + 1):
                                transposes(xn, QT0 + k, k, at)
                        if s == 2:
                            pe.wait_ge(ln_done, at(4, 6))
                            for k in range(4):
                                transposes(x3, XT0 + k, k, at)
                        if s == 3:
                            pe.wait_ge(*used(at, XT0 + 3))
                            logits(LG, at)
                            hidden(H0, 0, at)
                        if s == 4:
                            hidden(H0 + 1, 1, at)
                        if s == 5:
                            pe.wait_ge(*used(at, H0 + 1))
                            for n in range(NT):
                                hidden_transposes(HT0 + n, n, at)
                            pe.wait_ge(v_done, at(2, 4))
                        if s in (5, 6):
                            for k in (2 * s - 10, 2 * s - 9):
                                transposes(kv, KT0 + k, k, at)
                        if s == 6:
                            pe.wait_ge(*used(at, HT0 + 1))
                        if s >= 6:
                            expert_out(Y0 + s - 6, s - 6, at)
                        if s == 8:
                            expert_out(Y0 + 3, 3, at)
                        if s >= 1:
                            t = s - 1
                            if t == 0:
                                pe.wait_ge(v_done, at(2, 2))
                            pe.wait_ge(y_done, at(NPAIR, t + 1))
                            for e in range(2):
                                pe.wait_ge(pT_done, at(H, 2 * t + e + 1))
                                last = weights_times_values(
                                    pe, ps_o[:, e], lambda i, k: probT[:, e, i, bass.ts(k, P)],
                                    v[:, b], 2 * t + e)
                            last.then_inc(o_ready, 1)
            at = after_rounds
            pe.wait_ge(ln_done, at(4, 6))
            for k in range(4):
                transposes(x3, k, k, at)
            pe.wait_ge(*used(at, 3))
            logits(4, at)
            hidden(5, 0, at)
            hidden(6, 1, at)
            pe.wait_ge(*used(at, 6))
            for n in range(NT):
                hidden_transposes(7 + n, n, at)
            pe.wait_ge(*used(at, 8))
            for j in range(4):
                expert_out(LAST_Y + j, j, at)

        @block.scalar
        def _(act):
            def high(dst, c, at):
                act.wait_ge(j_ready, ready(at, c))
                act.activation(dst, bank_of(c)[:], ACT.Copy).then_inc(hi_done, 1)

            def values(slot, wanted):
                act.wait_ge(ctx_in, wanted)
                for n in range(NT):
                    act.activation(v[:, slot, 0, n, :, 0:HD],
                                   kv[:, n].rearrange("p (h d) -> p h d", d=HD),
                                   ACT.Copy).then_inc(v_hi, 1)

            def gate_exp(wanted):
                act.wait_ge(gating, wanted)
                act.activation(gexp[:], gap[:], ACT.Exp).then_inc(gap_exp, 1)

            def norm_apply(dst, src, wanted):
                act.wait_ge(ln_pow, wanted)
                for a in range(NT):
                    act.activation(dst[:, a, :], src[:, a, :], ACT.Identity,
                                   scale=rstd[:, a:a + 1], bias=offset[:, a:a + 1]) \
                        .then_inc(ln_done, 1)

            act.sem_inc(exp_done, 2)
            norm_apply(xn, xn, 2)
            for c in range(FIRST):
                act.wait_ge(j_ready, c + 1)
                k = c % 4
                act.activation((kT, qT)[c // 4][:, 0, 0, 2 * k:2 * k + 2, :], bank_of(c)[:],
                               ACT.Copy).then_inc(hi_done, 1)
            values(0, 16)
            norm_apply(xn, xn, 4)
            with act.Fori(0, NB // 2) as i:
                for b in range(2):
                    at = in_round(i, b)
                    for s in range(NSTEP):
                        halved = {0: (("q", 0), ("q", 1)), 1: (("q", 2), ("q", 3)),
                                  2: [("x", k) for k in range(4)],
                                  5: (("h", 0), ("h", 1), ("k", 0), ("k", 1)),
                                  6: (("k", 2), ("k", 3))}.get(s, ())

                        def large(which, k):
                            a = slice(2 * k, 2 * k + 2)
                            if which == "q":
                                high(qT[:, 1 - b, 0, a, :], QT0 + k, at)
                            if which == "x":
                                high(x3T[:, 0, a, :], XT0 + k, at)
                            if which == "h":
                                high(hT[:, 0, k], HT0 + k, at)
                            if which == "k":
                                high(kT[:, 1 - b, 0, a, :], KT0 + k, at)

                        if s >= 1:
                            for e in range(2):
                                act.wait_ge(pT_ready, at(H, 2 * (s - 1) + e + 1))
                                act.activation(probT[:, e, 0, :], ps_t[e][:, 0:3 * P], ACT.Copy) \
                                    .then_inc(pT_hi, 1)
                        early = 1 if s > 0 else 0
                        for which, k in halved[:early]:
                            large(which, k)
                        if s < NPAIR:
                            for e in range(2):
                                h = 2 * s + e
                                act.wait_ge(max_done, at(2 * H, 2 * h + 2))
                                act.activation(prob[:, h % 4, 0:P], ps_s[e][:, 0:P], ACT.Exp,
                                               bias=negmax[:, h % 4, 0:1])
                                act.activation(prob[:, h % 4, P:3 * P], ps_s[e][:, P:3 * P],
                                               ACT.Exp, bias=negmax[:, h % 4, 1:2]) \
                                    .then_inc(exp_done, 1)
                        for which, k in halved[early:]:
                            large(which, k)
                        if s == 1:
                            norm_apply(x3, x2[:, 1 - b], at(4, 6))
                        if s == 3:
                            gate_exp(at(8, 2))
                            values(1 - b, at(16, 32))
                        if s == 5:
                            norm_apply(xn, xn, at(4, 8))
            at = after_rounds
            norm_apply(x3, x2[:, 1], at(4, 6))
            for k in range(4):
                high(x3T[:, 0, 2 * k:2 * k + 2, :], k, at)
            gate_exp(at(8, 2))
            for n in range(NT):
                high(hT[:, 0, n], 7 + n, at)

        @block.gpsimd
        def _(pool):
            def reciprocal_root(wanted, halfway):
                pool.wait_ge(ln_stat, wanted)
                pool.tensor_tensor(rstd[:], rstd[:], minus_half[:], ALU.pow) \
                    .then_inc(ln_pow, 1)
                pool.wait_ge(ln_pow, halfway)
                pool.tensor_tensor(offset[:], minus_mean[:], rstd[:], ALU.mult) \
                    .then_inc(ln_pow, 1)

            def values(slot, wanted):
                for n in range(NT):
                    pool.wait_ge(v_hi, wanted[n])
                    pool.tensor_tensor(v[:, slot, 1, n, :, 0:HD],
                                       kv[:, n].rearrange("p (h d) -> p h d", d=HD),
                                       v[:, slot, 0, n, :, 0:HD], ALU.subtract) \
                        .then_inc(v_done, 1)

            pool.memset(minus_half[:], -0.5).then_inc(zeroed, 1)
            for b in range(2):
                pool.memset(v[:, b, 0, :, :, HD:HD + 1], 1.0).then_inc(zeroed, 1)
                pool.memset(v[:, b, 1, :, :, HD:HD + 1], 0.0).then_inc(zeroed, 1)
            pool.wait_ge(zeroed, 5)
            pool.sem_inc(x2_done, 1)
            reciprocal_root(8, 1)
            values(0, (1, 2))
            reciprocal_root(16, 3)
            with pool.Fori(0, NB // 2) as i:
                for b in range(2):
                    at = in_round(i, b)
                    reciprocal_root(at(16, 24), at(4, 5))
                    pool.wait_ge(x1_in, at(16, 16))
                    for t in range(NPAIR):
                        pool.wait_ge(y_done, at(NPAIR, 1 + t + 1))
                        pair = bass.ts(t, P)
                        pool.tensor_tensor(x2[:, b, :, pair], x2[:, b, :, pair],
                                           x1[:, b, :, pair], ALU.add).then_inc(x2_done, 1)
                        if t == 1:
                            values(1 - b, (at(2, 3), at(2, 4)))
                        if t == 2:
                            reciprocal_root(at(16, 32), at(4, 7))
            reciprocal_root(after_rounds(16, 24), after_rounds(4, 5))

        @block.vector
        def _(dve):
            def norm_stats(src, k, applied, divisor=1.0):
                for a in range(NT):
                    tile_stats(src, a)
                norm_sums(k, applied, divisor=divisor)

            def half_stats(slot, j):
                for a in range(NT):
                    dve.bn_stats(stats_x2[:, a, j, :], x2[:, slot, a, bass.ts(j, BANK)]) \
                        .then_inc(ln_stat, 1)

            def tile_stats(src, a):
                for j in range(2):
                    dve.bn_stats(stats[:, a, j, :], src[:, a, bass.ts(j, BANK)]) \
                        .then_inc(ln_stat, 1)

            def norm_sums(k, applied, stats=stats, divisor=1.0):
                if applied is not None:
                    dve.wait_ge(ln_done, applied)
                dve.wait_ge(ln_stat, k(4))
                dve.memset(nothing[:], 0.0)
                for a in range(NT):
                    dve.bn_aggr(mv[:, a, :], stats[:, a]).then_inc(ln_stat, 1)
                dve.wait_ge(ln_stat, k(6))
                dve.tensor_scalar(rstd[:], mv[:, :, 1], LN_EPS, divisor * divisor, ALU.add,
                                  ALU.mult).then_inc(ln_stat, 1)
                dve.tensor_scalar(minus_mean[:], mv[:, :, 0], -1.0, None, ALU.mult) \
                    .then_inc(ln_stat, 1)

            def low(dst, hi, c, k, at):
                dve.wait_ge(hi_done, at(NHI, FIRST + k + 1))
                src = bank_of(c)[:].rearrange("p (a n) -> p a n", a=hi.shape[1])
                dve.tensor_tensor(dst, src, hi, ALU.subtract).then_inc(j_free[c % NJ], 1)

            def add_expert_out(c, j, slot, at):
                n, half = j // 2, j % 2
                z = x2[:, slot, n, bass.ts(half, BANK)]
                dve.wait_ge(j_ready, ready(at, c))
                dve.scalar_tensor_tensor(z, bank_of(c)[:], 1.0 / (E_SCALE * R), z,
                                         ALU.mult, ALU.add).then_inc(j_free[c % NJ], 1)

            def gate_first(c, at):
                dve.wait_ge(j_ready, ready(at, c))
                dve.scalar_tensor_tensor(
                    logit[:], bank_of(c)[:, 0:NT * E].rearrange("p (n e) -> p n e", n=NT),
                    1.0 / E_SCALE, bias[:].unsqueeze(1).broadcast_to([P, NT, E]),
                    ALU.mult, ALU.add).then_inc(j_free[c % NJ], 1)
                dve.wait_ge(*used(at, c))
                dve.tensor_reduce(top[:], logit[:], AX.X, ALU.max).then_inc(gating, 1)
                dve.wait_ge(gating, at(8, 1))
                dve.tensor_tensor(gap[:], logit[:], top[:].unsqueeze(2).broadcast_to([P, NT, E]),
                                  ALU.subtract).then_inc(gating, 1)
                dve.wait_ge(gating, at(8, 2))
                dve.scalar_tensor_tensor(rank[:], gap[:], 0.0,
                                         order[:].unsqueeze(1).broadcast_to([P, NT, E]),
                                         ALU.is_equal, ALU.mult).then_inc(gating, 1)
                dve.wait_ge(gating, at(8, 3))
                dve.tensor_reduce(best[:], rank[:], AX.X, ALU.max).then_inc(gating, 1)

            def gate_second(n_exp, at):
                dve.wait_ge(gap_exp, n_exp)
                dve.tensor_reduce(total[:], gexp[:], AX.X, ALU.add).then_inc(gating, 1)
                dve.wait_ge(gating, at(8, 5))
                dve.reciprocal(weight[:], total[:]).then_inc(gating, 1)
                dve.tensor_tensor(onehot[:], rank[:], best[:].unsqueeze(2).broadcast_to([P, NT, E]),
                                  ALU.is_equal).then_inc(gating, 1)
                dve.wait_ge(gating, at(8, 7))
                dve.scalar_tensor_tensor(gate[:], onehot[:], 1.0 / E_SCALE,
                                         weight[:].unsqueeze(2).broadcast_to([P, NT, E]),
                                         ALU.mult, ALU.mult).then_inc(gating, 1)

            def gated(c, n, at):
                dve.wait_ge(j_ready, ready(at, c))
                if n == 0:
                    dve.wait_ge(gating, at(8, 8))
                dve.tensor_tensor(hg[:, n].rearrange("p (e r) -> p e r", e=E),
                                  bank_of(c)[:].rearrange("p (e r) -> p e r", e=E),
                                  gate[:, n].unsqueeze(2).broadcast_to([P, E, R]),
                                  ALU.mult).then_inc(j_free[c % NJ], 1)

            dve.sem_inc(y_done, 1)
            dve.memset(x2[:, 1], 0.0).then_inc(x2_zero, 1)
            dve.wait_ge(xn_in, 16)
            norm_stats(xn, lambda k: k, None, HD ** 0.5)
            for c in range(FIRST):
                k = slice(2 * (c % 4), 2 * (c % 4) + 2)
                dst = (kT, qT)[c // 4]
                dve.wait_ge(hi_done, c + 1)
                dve.tensor_tensor(dst[:, 0, 1, k, :],
                                  bank_of(c)[:].rearrange("p (a n) -> p a n", a=2),
                                  dst[:, 0, 0, k, :], ALU.subtract).then_inc(j_free[c % NJ], 1)
            dve.wait_ge(x2_zero, 1)
            dve.wait_ge(xn_in, 32)
            norm_stats(xn, lambda k: 8 + k, 2, HD ** 0.5)
            half_stats(1, 0)
            with dve.Fori(0, NB // 2) as i:
                for b in range(2):
                    at = in_round(i, b)
                    for s in range(NSTEP):
                        if s < NPAIR:
                            for e in range(2):
                                h = 2 * s + e
                                dve.wait_ge(s_ready, at(H, h + 1))
                                for n, cols in enumerate((slice(0, P), slice(P, 3 * P))):
                                    dve.tensor_reduce(negmax[:, h % 4, n:n + 1], ps_s[e][:, cols],
                                                      AX.X, ALU.max, negate=True) \
                                        .then_inc(max_done, 1)
                        if s >= 1:
                            for e in range(2):
                                dve.wait_ge(pT_hi, at(H, 2 * (s - 1) + e + 1))
                                dve.tensor_tensor(probT[:, e, 1, :], ps_t[e][:, 0:3 * P],
                                                  probT[:, e, 0, :], ALU.subtract) \
                                    .then_inc(pT_done, 1)
                        if s == 0:
                            dve.wait_ge(x2_done, at(NPAIR, 1))
                            half_stats(1 - b, 1)
                        if s <= 1:
                            for k in (2 * s, 2 * s + 1):
                                a = slice(2 * k, 2 * k + 2)
                                low(qT[:, 1 - b, 1, a, :], qT[:, 1 - b, 0, a, :], QT0 + k, k,
                                    at)
                        if s == 0:
                            norm_sums(lambda k: at(16, 16 + k), at(4, 4), stats_x2)
                        if s == 2:
                            for k in range(4):
                                a = slice(2 * k, 2 * k + 2)
                                low(x3T[:, 1, a, :], x3T[:, 0, a, :], XT0 + k, 4 + k, at)
                        if s == 3:
                            gate_first(LG, at)
                            gate_second(at(1, 1), at)
                            dve.wait_ge(xn_in, at(16, 48))
                            tile_stats(xn, 0)
                            gated(H0, 0, at)
                        if s == 4:
                            tile_stats(xn, 1)
                            norm_sums(lambda k: at(16, 24 + k), at(4, 6), divisor=HD ** 0.5)
                            gated(H0 + 1, 1, at)
                        if s == 5:
                            for n in range(NT):
                                low(hT[:, 1, n], hT[:, 0, n], HT0 + n, 8 + n, at)
                        if s in (5, 6):
                            for k in (2 * s - 10, 2 * s - 9):
                                a = slice(2 * k, 2 * k + 2)
                                low(kT[:, 1 - b, 1, a, :], kT[:, 1 - b, 0, a, :], KT0 + k, 10 + k,
                                    at)
                        if s >= 6:
                            add_expert_out(Y0 + s - 6, s - 6, 1 - b, at)
                        if s == 8:
                            add_expert_out(Y0 + 3, 3, 1 - b, at)
                        if s >= 1:
                            t = s - 1
                            dve.wait_ge(o_ready, at(NPAIR, t + 1))
                            dve.reciprocal(rinv[:], ps_o[:, :, :, HD]).then_inc(recip_done, 1)
                            if t == 0:
                                dve.wait_ge(out_done, at(16, 16))
                            dve.wait_ge(recip_done, at(NPAIR, t + 1))
                            dve.tensor_tensor(
                                x2[:, b, :, bass.ts(t, P)].rearrange("p n (e d) -> p e n d", e=2),
                                ps_o[:, :, :, 0:HD],
                                rinv[:].unsqueeze(3).broadcast_to([P, 2, NT, HD]),
                                ALU.mult).then_inc(y_done, 1)
                        if s == 7:
                            dve.wait_ge(x2_done, at(NPAIR, 1 + NPAIR // 2))
                            half_stats(b, 0)
            at = after_rounds
            dve.wait_ge(x2_done, at(NPAIR, 1))
            half_stats(1, 1)
            norm_sums(lambda k: at(16, 16 + k), at(4, 4), stats_x2)
            for k in range(4):
                a = slice(2 * k, 2 * k + 2)
                low(x3T[:, 1, a, :], x3T[:, 0, a, :], k, k, at)
            gate_first(4, at)
            gate_second(at(1, 1), at)
            gated(5, 0, at)
            gated(6, 1, at)
            for n in range(NT):
                low(hT[:, 1, n], hT[:, 0, n], 7 + n, 4 + n, at)
            for j in range(4):
                add_expert_out(LAST_Y + j, j, 1, at)


LAST_Y = 9


def expert_weights(nc, ident, ps, aT, bT, rT, bias, order, A, B, Wr, br, early):
    with ExitStack() as st:
        a_in = st.enter_context(nc.sbuf_tensor("a_in", [P, ERT, D], F32))
        b_in = st.enter_context(nc.sbuf_tensor("b_in", [P, DT, ER], F32))
        r_in = st.enter_context(nc.sbuf_tensor("r_in", [E, D], F32))
        loaded = [st.enter_context(nc.semaphore(f"{n}_in_sem")) for n in ("b", "r", "bias")]
        a_loaded = [st.enter_context(nc.semaphore(f"a_loaded{k}")) for k in range(ERT)]
        early_in = st.enter_context(nc.semaphore("early_in2"))
        moved = st.enter_context(nc.semaphore("moved"))
        hi_kept = st.enter_context(nc.semaphore("hi_kept"))
        lo_kept = st.enter_context(nc.semaphore("lo_kept"))
        block = st.enter_context(nc.Block())

        def place(c):
            if c < 2 * ERT:
                k, j = c // 2, c % 2
                return [aT[:, i, 4 * j:4 * j + 4, bass.ts(k, P)] for i in range(2)]
            if c < 2 * ERT + DT:
                return [bT[:, i, :, bass.ts(c - 2 * ERT, P)] for i in range(2)]
            return [rT[:, i] for i in range(2)]

        def product(c):
            n = DT * E if c == 2 * ERT + DT else BANK
            return ps[c % NJ][:, 0:n].rearrange("p (a n) -> p a n", a=DT if n < BANK else 4)

        @block.sync
        def _(sp):
            rows = A.rearrange("e r d -> (e r) d")
            for k in range(ERT):
                sp.dma_start(a_in[:, k], rows[k * P:k * P + P]).then_inc(a_loaded[k], 16)
            for k in range(DT):
                sp.dma_start(b_in[:, k].rearrange("p (e r) -> p e r", e=E),
                             B[:, k * P:k * P + P, :].rearrange("e p r -> p e r")) \
                    .then_inc(loaded[0], 16)
            sp.dma_start(r_in[:], Wr).then_inc(loaded[1], 16)
            sp.dma_start(bias[:], br.partition_broadcast(P)).then_inc(loaded[2], 16)
            for to, source in early:
                sp.dma_start(to, source).then_inc(early_in, 16)
            sp.wait_ge(loaded[2], 16)
            sp.wait_ge(early_in, 16 * len(early))

        @block.gpsimd
        def _(pool):
            for e in range(E):
                pool.memset(order[:, e:e + 1], float(E - e))

        @block.tensor
        def _(pe):
            for c in range(2 * ERT + DT + 1):
                if c >= NJ:
                    pe.wait_ge(lo_kept, c - NJ + 1)
                if c < 2 * ERT:
                    k, j = c // 2, c % 2
                    if j == 0:
                        pe.wait_ge(a_loaded[k], 16)
                    for a in range(4):
                        last = pe.transpose(ps[c % NJ][:, bass.ts(a, P)],
                                            a_in[:, k, bass.ts(4 * j + a, P)], ident[:])
                elif c < 2 * ERT + DT:
                    if c == 2 * ERT:
                        pe.wait_ge(loaded[0], 16 * DT)
                    for a in range(ERT):
                        last = pe.transpose(ps[c % NJ][:, bass.ts(a, P)],
                                            b_in[:, c - 2 * ERT, bass.ts(a, P)], ident[:])
                else:
                    pe.wait_ge(loaded[1], 16)
                    for a in range(DT):
                        last = pe.transpose(ps[c % NJ][:, bass.ts(a, E)],
                                            r_in[:, bass.ts(a, P)], ident[0:E, 0:E])
                last.then_inc(moved, 1)

        @block.scalar
        def _(act):
            for c in range(2 * ERT + DT + 1):
                act.wait_ge(moved, c + 1)
                act.activation(place(c)[0], product(c), ACT.Copy, scale=E_SCALE) \
                    .then_inc(hi_kept, 1)

        @block.vector
        def _(dve):
            for c in range(2 * ERT + DT + 1):
                dve.wait_ge(hi_kept, c + 1)
                dve.scalar_tensor_tensor(place(c)[1], product(c), E_SCALE, place(c)[0],
                                         ALU.mult, ALU.subtract).then_inc(lo_kept, 1)


def rope_tables():
    half = HD // 2
    freq = (np.float32(1) / np.float32(10000) ** (np.arange(half, dtype=np.float32)
                                                  / np.float32(half))).astype(np.float32)
    angle = np.outer(freq, np.arange(T, dtype=np.float32)).astype(np.float64)
    cos = np.tile(np.cos(angle), (4, 1))
    sin = np.concatenate([-np.sin(angle), np.sin(angle)] * 2)
    scales = np.array([HD ** -0.5, 1.0])
    return tuple((t[:, None, :] * scales[None, :, None]).astype(np.float32) for t in (cos, sin))


INPUTS = ("x", "ctx_2048", "L0_attn_w_q", "L0_attn_w_k", "L0_attn_w_v", "L0_attn_w_o",
          "L0_ffn_A", "L0_ffn_B", "L0_ffn_Wr", "L0_ffn_br")


def kernel(**inputs):
    import concourse.bacc as bacc
    from concourse.bass_utils import run_bass_kernel_spmd

    nc = bacc.Bacc("TRN2", target_bir_lowering=False, num_devices=1)
    cos, sin = rope_tables()
    arrays = {"in_" + name: np.ascontiguousarray(inputs[name]) for name in INPUTS}
    arrays["rope_cos"], arrays["rope_sin"] = cos, sin
    aps = [nc.dram_tensor(name, a.shape, F32, kind="ExternalInput").ap()
           for name, a in arrays.items()]
    out = nc.dram_tensor("out", (NB, T, D), F32, kind="ExternalOutput").ap()
    program(nc, *aps, out)
    result = run_bass_kernel_spmd(nc, [arrays], core_ids=[0])
    return result.results[0]["out"]
```
